# Optimizing a Trainium2 kernel written in Bass

```python
import numpy as np
import jax
import jax.numpy as jnp

def _softmax(x, axis=-1):
    return jax.nn.softmax(x, axis=axis)

def _gelu(x):
    return jax.nn.gelu(x, approximate=True)

def _silu(x):
    return jax.nn.silu(x)

def _sigmoid(x):
    return jax.nn.sigmoid(x)

def _layernorm(x, axis=-1, eps=1e-05):
    m = jnp.mean(x, axis=axis, keepdims=True)
    v = jnp.var(x, axis=axis, keepdims=True)
    return (x - m) / jnp.sqrt(v + eps)

def _scatter_add(tgt, idx, src, axis=0):
    return tgt.at[idx].add(src)

def _segment_sum(src, seg, n):
    return jax.ops.segment_sum(src, seg, n)
kernel_name = 'mk_adaln_d1_jaxref_r8_c2e7fd'

def setup_inputs(seed: int=0):
    np.random.seed(seed)
    _w = jnp.asarray

    def _L0_attn_setup():
        import jax, jax.numpy as jnp
        import numpy as np
        B, L, C = (2, 512, 128)
        H, WIN = (16, 128)
        D = C // H
        key = jax.random.key(seed)
        ks = jax.random.split(key, 9)
        s = 0.02
        return {'x': jax.random.normal(ks[0], (B, L, C), jnp.float32), 'wq': jax.random.normal(ks[1], (C, C), jnp.float32) * s, 'bq': jnp.zeros((C,), jnp.float32), 'wk': jax.random.normal(ks[2], (C, C), jnp.float32) * s, 'bk': jnp.zeros((C,), jnp.float32), 'wv': jax.random.normal(ks[3], (C, C), jnp.float32) * s, 'bv': jnp.zeros((C,), jnp.float32), 'wo': jax.random.normal(ks[4], (C, C), jnp.float32) * s, 'bo': jnp.zeros((C,), jnp.float32)}
    _L0_attn_in = _L0_attn_setup()

    def _L0_ffn_setup():
        import jax, jax.numpy as jnp
        import numpy as np
        W_SCALE = 0.02
        TOP_K = 2
        key = jax.random.key(seed)
        ks = jax.random.split(key, 5)
        B, S, H, I, E = (2, 128, 128, 512, 8)
        return {'x': jax.random.normal(ks[0], (B, S, H), dtype=jnp.float32), 'gate': jax.random.normal(ks[1], (H, E), dtype=jnp.float32) * W_SCALE, 'experts_w1': jax.random.normal(ks[2], (E, H, I), dtype=jnp.float32) * W_SCALE, 'experts_w2': jax.random.normal(ks[3], (E, I, H), dtype=jnp.float32) * W_SCALE, 'experts_w3': jax.random.normal(ks[4], (E, H, I), dtype=jnp.float32) * W_SCALE}
    _L0_ffn_in = _L0_ffn_setup()
    _L0_c = _w((lambda *s: np.random.randn(*s).astype(np.float32) * 0.05)(8, 128))
    _L0_wmod = _w((lambda *s: np.random.randn(*s).astype(np.float32) * 0.05)(128, 6 * 128) * 128 ** (-0.5))
    _d = {'L0_attn_x': _L0_attn_in['x'], 'L0_attn_wq': _L0_attn_in['wq'], 'L0_attn_bq': _L0_attn_in['bq'], 'L0_attn_wk': _L0_attn_in['wk'], 'L0_attn_bk': _L0_attn_in['bk'], 'L0_attn_wv': _L0_attn_in['wv'], 'L0_attn_bv': _L0_attn_in['bv'], 'L0_attn_wo': _L0_attn_in['wo'], 'L0_attn_bo': _L0_attn_in['bo'], 'L0_ffn_gate': _L0_ffn_in['gate'], 'L0_ffn_experts_w1': _L0_ffn_in['experts_w1'], 'L0_ffn_experts_w2': _L0_ffn_in['experts_w2'], 'L0_ffn_experts_w3': _L0_ffn_in['experts_w3'], 'L0_c': _L0_c, 'L0_wmod': _L0_wmod}
    _x0 = _d['L0_attn_x']
    _d['L0_attn_x'] = jax.random.normal(jax.random.fold_in(jax.random.key(seed), 1), (8, 256, 128), dtype=_x0.dtype)
    del _x0
    return _d

def reference(L0_attn_x, L0_attn_wq, L0_attn_bq, L0_attn_wk, L0_attn_bk, L0_attn_wv, L0_attn_bv, L0_attn_wo, L0_attn_bo, L0_ffn_gate, L0_ffn_experts_w1, L0_ffn_experts_w2, L0_ffn_experts_w3, L0_c, L0_wmod):

    def _L0_attn_ref(x, wq, bq, wk, bk, wv, bv, wo, bo):
        import jax, jax.numpy as jnp
        import numpy as np
        B, L, C = (2, 512, 128)
        H, WIN = (16, 128)
        D = C // H
        b, l, c = x.shape
        nb = l // WIN

        def heads(t):
            return t.reshape(b, l, H, D).transpose(0, 2, 1, 3)
        q = heads(x @ wq + bq)
        k = heads(x @ wk + bk)
        v = heads(x @ wv + bv)
        kp = jnp.pad(k, ((0, 0), (0, 0), (WIN, WIN), (0, 0)))
        vp = jnp.pad(v, ((0, 0), (0, 0), (WIN, WIN), (0, 0)))
        idx = np.arange(nb)[:, None] * WIN + np.arange(3 * WIN)[None, :]
        kb = kp[:, :, idx]
        vb = vp[:, :, idx]
        qb = q.reshape(b, H, nb, WIN, D)
        scores = jnp.einsum('bhnqd,bhnkd->bhnqk', qb, kb) / float(np.sqrt(D))
        r = np.arange(WIN)[:, None]
        col = np.arange(3 * WIN)[None, :]
        band = jnp.asarray(np.abs(col - r - WIN) <= WIN)
        scores = jnp.where(band, scores, -jnp.inf)
        probs = jax.nn.softmax(scores, axis=-1)
        out = jnp.einsum('bhnqk,bhnkd->bhnqd', probs, vb)
        out = out.reshape(b, H, l, D).transpose(0, 2, 1, 3).reshape(b, l, c)
        return out @ wo + bo

    def _L0_ffn_ref(x, gate, experts_w1, experts_w2, experts_w3):
        import jax, jax.numpy as jnp
        import numpy as np
        W_SCALE = 0.02
        TOP_K = 2
        E = experts_w1.shape[0]
        router_logits = jnp.einsum('bsh,he->bse', x, gate)
        routing_weights, selected = jax.lax.top_k(router_logits, TOP_K)
        routing_weights = jax.nn.softmax(routing_weights, axis=-1)
        onehot = jax.nn.one_hot(selected, E, dtype=x.dtype)
        tok_w = jnp.einsum('bsk,bske->bse', routing_weights, onehot)
        g = jnp.einsum('bsh,ehi->ebsi', x, experts_w1)
        u = jnp.einsum('bsh,ehi->ebsi', x, experts_w3)
        hid = jax.nn.silu(g) * u
        eo = jnp.einsum('ebsi,eih->ebsh', hid, experts_w2)
        out = jnp.einsum('ebsh,bse->bsh', eo, tok_w)
        return out
    x = L0_attn_x
    mod = (_silu(L0_c) @ L0_wmod).reshape(L0_c.shape[0], 6, 1, -1)
    sa, ca, ga, sb, cb, gb = (mod[:, 0], mod[:, 1], mod[:, 2], mod[:, 3], mod[:, 4], mod[:, 5])
    ga = (2 * (ga >= 0) - 1) * jnp.maximum(jnp.abs(ga), 0.25)
    gb = (2 * (gb >= 0) - 1) * jnp.maximum(jnp.abs(gb), 0.25)
    h = _layernorm(x, axis=-1) * (1 + ca) + sa
    x = x + ga * _L0_attn_ref(h, L0_attn_wq, L0_attn_bq, L0_attn_wk, L0_attn_bk, L0_attn_wv, L0_attn_bv, L0_attn_wo, L0_attn_bo)
    h = _layernorm(x, axis=-1) * (1 + cb) + sb
    x = x + gb * _L0_ffn_ref(h, L0_ffn_gate, L0_ffn_experts_w1, L0_ffn_experts_w2, L0_ffn_experts_w3)
    return x

_drawn_inputs = setup_inputs


def setup_inputs(seed=0):
    import zlib

    import numpy as np

    out = dict(_drawn_inputs(seed))
    spreads = {'L0_attn_bq': (0.0, 0.8),
     'L0_attn_bk': (0.0, 0.8),
     'L0_attn_bv': (0.0, 0.8),
     'L0_attn_bo': (0.0, 0.323)}
    factors = {'L0_attn_wq': 8.0,
     'L0_attn_wk': 8.0,
     'L0_attn_wv': 8.0,
     'L0_attn_wo': 8.0,
     'L0_ffn_gate': 8.0,
     'L0_ffn_experts_w1': 8.0,
     'L0_ffn_experts_w2': 8.0,
     'L0_ffn_experts_w3': 8.0}
    for name, (base, spread) in spreads.items():
        noise = np.random.default_rng([zlib.crc32(name.encode()), seed]).standard_normal(out[name].shape)
        drawn = base * np.exp(spread * noise) if base else spread * noise
        out[name] = jnp.asarray(drawn.astype(out[name].dtype))
    for name, factor in factors.items():
        out[name] = (out[name] * factor).astype(out[name].dtype)
    return out
```

```python
from contextlib import ExitStack

import numpy as np

import concourse.bass as bass
from concourse import mybir

P = 128
ALU = mybir.AluOpType
ACT = mybir.ActivationFunctionType
AX = mybir.AxisListType
F32 = mybir.dt.float32
BF16 = mybir.dt.bfloat16
I32 = mybir.dt.int32
U32 = mybir.dt.uint32

H2 = 2
D = 8
NPAIR = 8
QP = (0, 0, 0, 1, 1, 2)
KP = (0, 1, 2, 0, 1, 0)
NSLOT = len(QP)
HROWS = NSLOT * D
SROWS = H2 * HROWS
RING = 3
VRING = 4
AHEAD = 2
VCOL = 32
PRING = 8
MASKED = -1e30
EPS = 1e-5


def first(v):
    return isinstance(v, int) and v == 0


def adaln_attention_moe(nc, x, wq, bq, wk, bk, wv, bv, wo, bo, gate, w1, w2, w3, c, wmod, out):
    B, L, C = x.shape
    NT = B * L // P
    E, _, I = w1.shape
    NC = I // P
    NTOK = B * L
    TOPK = 2
    NTILE = (TOPK * NTOK - E) // P + E
    TRING = 3
    ROUND = 1.5 * 2.0 ** 23
    assert L == 2 * P and C == P and NTILE % TRING == 0

    with ExitStack() as ctx:
        def sb(name, shape, dt=F32):
            return ctx.enter_context(nc.sbuf_tensor(name, shape, dt))

        def sem(name):
            return ctx.enter_context(nc.semaphore(name))

        parts_d = nc.dram_tensor("parts_d", [B, 2, 3, P, L], BF16, kind="Internal").ap()
        mod_d = nc.dram_tensor("mod_d", [B, 5 * P], F32, kind="Internal").ap()
        h2_d = nc.dram_tensor("h2_d", [B * L, C], F32, kind="Internal").ap()

        y_d = nc.dram_tensor("y_d", [TOPK * NTOK + NTILE * P, C], F32, kind="Internal").ap()

        w1_sb = sb("w1_sb", [P, E, I])
        w3_sb = sb("w3_sb", [P, E, I])
        w2_sb = sb("w2_sb", [P, E, NC, C])
        tri = sb("tri", [P, P], BF16)
        ones_b = sb("ones_b", [P, P], BF16)
        iota_e = sb("iota_e", [P, E])
        iota_a = sb("iota_a", [P, NTILE])
        iota_c = sb("iota_c", [P, P], BF16)
        iota_p = sb("iota_p", [P, 1])
        iota_kt = sb("iota_kt", [P, TOPK * NT])
        dump_row = sb("dump_row", [P, NTILE])
        iotas = sb("iotas", [P, 256], I32)
        topf = sb("topf", [P, NT, TOPK])
        pick = sb("pick", [P, TOPK, NT, E], BF16)
        used = sb("used", [P, NT, E], BF16)
        before = sb("before", [P, NT + 1, E], BF16)
        ntile_e = sb("ntile_e", [P, 3, E])
        upto = sb("upto", [P, 4, 2 * E])
        gat_idx = sb("gat_idx", [P, NTILE], I32)
        sca_idx = sb("sca_idx", [P, NTILE], I32)
        te_cmp = sb("te_cmp", [1, NTILE, E])
        te_sum = sb("te_sum", [1, NTILE])
        tile_e = sb("tile_e", [1, NTILE], I32)
        wts = sb("wts", [P, 4, NT])
        gidx = [sb(f"gidx{r}", [P, 1], I32) for r in range(TRING)]
        sidx = [sb(f"sidx{r}", [P, 1], I32) for r in range(TRING)]
        x_sb = sb("x_sb", [P, NT, C])
        mod_sb = sb("mod_sb", [P, B, 5, C])
        ident = sb("ident", [P, P])
        ident_b = sb("ident_b", [P, P], BF16)
        mask_b = sb("mask_b", [P, 2, H2, P], BF16)
        c_sb = sb("c_sb", [B, C])
        cT = sb("cT", [P, 4, B])
        modrow = sb("modrow", [B, 7, C])
        bo8 = sb("bo8", [B, C])
        modT = sb("modT", [P, 2, B])
        wqk = sb("wqk", [P, 2, C])
        wv_sb = sb("wv_sb", [P, C])
        wo_sb = sb("wo_sb", [P, C])
        gate_sb = sb("gate_sb", [P, 8])
        bqk = sb("bqk", [P, 4])
        bv_sb = sb("bv_sb", [P, C])
        stats = sb("stats", [P, NT, 6])
        mv = sb("mv", [P, NT, 2])
        veps = sb("veps", [P, NT])
        rstd = sb("rstd", [P, NT])
        neghalf = sb("neghalf", [P, NT])
        xn = sb("xn", [P, 2, 2, C])
        hT = sb("hT", [P, L])
        qkf = sb("qkf", [P, 2, L])
        parts = sb("parts", [P, 2, 3, L], BF16)
        resid = sb("resid", [P, 2, L])
        qs = sb("qs", [P, RING, NPAIR, L], BF16)
        kd = sb("kd", [P, RING, H2, NPAIR, L], BF16)
        vx = sb("vx", [P, VRING, 2, NPAIR, H2, VCOL])
        negm = sb("negm", [P, 2, 2, H2, NPAIR])
        negmb = sb("negmb", [P, 2, 2, 2, H2, 4], BF16)
        mT = sb("mT", [8, 2, 2, L], BF16)
        emin = sb("emin", [P, 3, 2, 2, H2, 4])
        npad_i = sb("npad_i", [P, 2], I32)
        npad = sb("npad", [P, 2])
        probs = sb("probs", [P, 2, PRING, H2, L])
        oS = sb("oS", [P, 2, L])
        den = sb("den", [P, 3, 2, H2 * NPAIR])
        attn = sb("attn", [P, 2, C])
        aT = sb("aT", [P, L])
        t1 = sb("t1", [P, 2, C])
        stats2 = sb("stats2", [P, 2, 6])
        mv2 = sb("mv2", [P, 2, 2])
        ve2 = sb("ve2", [P, 2])
        rs2 = sb("rs2", [P, 2])
        xn2 = sb("xn2", [P, 2, C])
        h2m = sb("h2m", [P, 2, C])
        h2 = sb("h2", [P, 2, 2, C])
        h2T = sb("h2T", [P, L])
        lg = sb("lg", [P, NT, 8])
        top = sb("top", [P, NT, 8])
        topi = sb("topi", [P, NT, 8], U32)

        start = probs[:].rearrange("p k a h q -> p (k a h q)")
        wmod_sb = start[:, 0:6 * C]
        wraw = start[:, 6 * C:8 * C].rearrange("p (w c) -> p w c", c=C)

        routing = qs[:].rearrange("p r q t -> p (r q t)")
        used_routing = [0]

        def routing_buf(dt, *dims):
            n = int(np.prod(dims)) * (2 if dt == F32 else 1)
            v = routing[:, used_routing[0]:used_routing[0] + n]
            used_routing[0] += n
            v = v.bitcast(dt) if dt == F32 else v
            names = " ".join("abc"[:len(dims)])
            return v.rearrange(f"p ({names}) -> p {names}", **{k: d for k, d in zip("abc", dims)})

        place = routing_buf(F32, NT, E)
        picked = routing_buf(F32, TOPK, NT, E)
        pos = routing_buf(F32, 5, TOPK * NT)
        inv = routing_buf(F32, 5, NTILE)
        inv_rhs = routing_buf(BF16, 2, TOPK * NT, NTILE)
        inv_sel = routing_buf(BF16, TOPK * NT, NTILE)
        inv_lhs = routing_buf(BF16, 4, P)

        moe = kd[:].rearrange("p r h q t -> p (r h q t)").bitcast(F32)
        used_moe = [0]

        def moe_buf(n):
            v = moe[:, used_moe[0]:used_moe[0] + n]
            used_moe[0] += n
            return v

        xs = moe_buf(TRING * C).rearrange("p (r c) -> p r c", c=C)
        xsT = moe_buf(TRING * P).rearrange("p (r c) -> p r c", c=P)
        ys = moe_buf(TRING * C).rearrange("p (r c) -> p r c", c=C)
        gate_act = moe_buf(TRING * I).rearrange("p (r i) -> p r i", i=I)
        hid = moe_buf(TRING * I).rearrange("p (r i) -> p r i", i=I)
        ybuf = probs[:].rearrange("p k a h q -> p (k a h q)")
        w1_t, w3_t, w2_t = (ybuf[:, i * TRING * I:(i + 1) * TRING * I].rearrange("c (r i) -> c r i", i=I) for i in range(3))
        y01 = ybuf[:, 0:TOPK * NT * C].rearrange("p (k t c) -> p k t c", k=TOPK, c=C)
        comb = ybuf[:, TOPK * NT * C:(TOPK + 1) * NT * C].rearrange("p (t c) -> p t c", c=C)
        outb = ybuf[:, (TOPK + 1) * NT * C:(TOPK + 2) * NT * C].rearrange("p (t c) -> p t c", c=C)

        psA = ctx.enter_context(nc.psum_tensor("psA", [P, 2, 2, 512], F32))
        psB = ctx.enter_context(nc.psum_tensor("psB", [P, 2, 512], F32))
        psO = ctx.enter_context(nc.psum_tensor("psO", [P, 2, L], F32))
        psM = ctx.enter_context(nc.psum_tensor("psM", [P, 512], F32))

        psG, psU = (psA[:, 0, 0, :], psA[:, 1, 0, :], psB[:, 0, :]), (psA[:, 0, 1, :], psA[:, 1, 1, :], psB[:, 1, :])
        psX, psY = psO[:, 0, 0:P], psM[:, 0:C]
        psR = psB[:, 1, :]

        gathered = [sem(f"gathered{r}") for r in range(TRING)]
        scattered = [sem(f"scattered{r}") for r in range(TRING)]
        s = {n: sem(n) for n in (
            "moe_w route_const iota_steps picks_ready rank_ps pos_steps lhs_ready lhs_used inv_ps idx_ready te_ready wt_steps wt_exp "
            "gidx_first gidx_next sidx_ready xsT_ps xsT_ready g_ps u_ps silu_ready hid_ready w1_ready w3_ready w2_ready y_ps y_ready "
            "y_in0 y_in1 y_in2 y_in3 y0_scaled comb_steps out_ready out_stored "
            "x_in0 x_in1 x_in2 c_in wmod_in0 wmod_in1 w_in wo_in consts masks cT_ps e_c silu_c silu_steps modT_ps modrow_ps modT_ok mod_steps mod_stored mod_in wqk_ok "
            "ln1_steps veps_ok rstd_ok stack_zero vx_const "
            "xn_ready xnT_ps hT_ready qk_ps qkf_ready part_cast residuals parts_stored v_ps v_ready "
            "scoresA rowmax half_max mT_ps mT_ready emin_ready m_in0 m_in1 "
            "scoresB exped masked pv o_ready oT_ps den_steps normed aT_ps aT_ready op_ps t1_ready xg_ready x1_ready "
            "ln2_steps rs2_ready xn2_ready h2m_ready h2_ready h2T_ps h2T_ready lg_ps lg_ready top_ready h2_stored0 h2_stored1 dbg_out"
        ).split()}
        stack_in = [sem(f"stack_in{i}") for i in range(RING)]
        block = ctx.enter_context(nc.Block())

        tok = lambda ap: ap.rearrange("b (t p) c -> p (b t) c", p=P)
        rounds = NTILE // TRING - 1
        NLOADS = 2 * 2 * 3

        @block.sync
        def _(sp):
            xt = tok(x)
            for i, (lo, hi) in enumerate(((0, 2), (2, 6), (6, NT))):
                sp.dma_start(x_sb[:, lo:hi, :], xt[:, lo:hi, :]).then_inc(s[f"x_in{i}"], 16)
            sp.dma_start(bv_sb[:], bv.partition_broadcast(P)).then_inc(s["w_in"], 16)
            for i, bias in enumerate((bq, bk)):
                for h in range(H2):
                    sp.dma_start(bqk[64 * h:64 * h + 64, i:i + 1],
                                 bias.rearrange("(p h d o) -> h d p o", p=NPAIR, h=H2, o=1)[h],
                                 allow_slow_non_contiguous=True).then_inc(s["w_in"], 16)
            sp.dma_start(wo_sb[:], wo).then_inc(s["wo_in"], 16)
            sp.dma_start(gate_sb[:], gate).then_inc(s["wo_in"], 16)
            sp.dma_start(w1_sb[:], w1.rearrange("e c i -> c e i")).then_inc(s["moe_w"], 16)
            sp.dma_start(w3_sb[:], w3.rearrange("e c i -> c e i")).then_inc(s["moe_w"], 16)
            sp.dma_start(w2_sb[:].rearrange("p e k c -> p (e k) c"), w2.rearrange("e (k p) c -> p (e k) c", p=P)).then_inc(s["moe_w"], 16)
            sp.wait_ge(s["stack_zero"], 4)
            def store_max(b, half):
                sp.wait_ge(s["mT_ready"], 2 * b + half + 1)
                sp.dma_start(qs[SROWS:SROWS + H2, b % RING, 4 * half:4 * half + 4, :],
                             mT[:, b % 2, half, :]).then_inc(s[f"m_in{half}"], 16)

            def store_parts(b):
                sp.wait_ge(s["residuals"], 3 * b + 3)
                sp.dma_start(parts_d[b].rearrange("w s c t -> c (w s) t"),
                             parts[:].rearrange("c w s t -> c (w s) t")).then_inc(s["parts_stored"], 16)

            def fill_stacks(b):
                sp.wait_ge(s["parts_stored"], 16 * b + 16)
                if b >= RING:
                    sp.wait_ge(s["scoresB"], 16 * (b - RING + 1))
                r = b % RING
                for h in range(H2):
                    q_src, k_src = (parts_d[b, side].rearrange("s (h d p) t -> h s d (p t)", h=H2, d=D)[h] for side in range(2))
                    q_dst = qs[h * HROWS:(h + 1) * HROWS, r].rearrange("r p t -> r (p t)")
                    k_dst = kd[h * HROWS:(h + 1) * HROWS, r, h].rearrange("r p t -> r (p t)")
                    for slot, n in ((0, 3), (3, 2), (5, 1)):
                        part = QP[slot]
                        sp.dma_start(q_dst[slot * D:(slot + n) * D],
                                     q_src[part:part + 1].broadcast_to([n, D, NPAIR * L])).then_inc(stack_in[r], 16)
                        sp.dma_start(k_dst[slot * D:(slot + n) * D], k_src[0:n]).then_inc(stack_in[r], 16)

            def broadcast_mod_rows():
                sp.wait_ge(s["mod_steps"], 7)
                sp.dma_start(mod_d, modrow[:, 0:5, :].rearrange("b r c -> b (r c)")).then_inc(s["mod_stored"], 16)
                sp.wait_ge(s["mod_stored"], 16)
                sp.dma_start(mod_sb[:].rearrange("p b r c -> p (b r c)"),
                             mod_d.rearrange("b r -> (b r)").partition_broadcast(P)).then_inc(s["mod_in"], 16)
            for step in range(-AHEAD, B + 4):
                if step == 1:
                    broadcast_mod_rows()
                if 0 <= step - 1 < B:
                    store_max(step - 1, 1)
                if 0 <= step + AHEAD - 1 < B:
                    fill_stacks(step + AHEAD - 1)
                if 0 <= step + AHEAD < B:
                    store_parts(step + AHEAD)
                if 0 <= step < B:
                    store_max(step, 0)
                if 0 <= step - 3 < B:
                    a = step - 3
                    sp.wait_ge(s["h2_ready"], a + 1)
                    sp.dma_start(h2_d.rearrange("(b t p) c -> b p t c", t=2, p=P)[a], h2[:, a % 2]).then_inc(s[f"h2_stored{a % 2}"], 16)
            for i in range(2):
                sp.wait_ge(s[f"h2_stored{i}"], 16 * (B // 2))
            for r in range(TRING):
                sp.wait_ge(scattered[r], 16 * (NTILE // TRING))
            n = NT // 4
            y_t = y_d[0:TOPK * NTOK].rearrange("(k t p) c -> p k t c", k=TOPK, p=P)
            for i in range(4):
                for k in range(TOPK):
                    sp.dma_start(y01[:, k, n * i:n * i + n], y_t[:, k, n * i:n * i + n]).then_inc(s[f"y_in{i}"], 16)
            for i in range(4):
                sp.wait_ge(s["out_ready"], i + 1)
                sp.dma_start(tok(out)[:, n * i:n * i + n], outb[:, n * i:n * i + n]).then_inc(s["out_stored"], 16)
            sp.wait_ge(s["out_stored"], 64)

        @block.scalar
        def _(act):
            act.dma_start(c_sb[:], c).then_inc(s["c_in"], 16)
            act.dma_start(wmod_sb[:, 0:2 * C], wmod[:, 0:2 * C]).then_inc(s["wmod_in0"], 16)
            act.dma_start(wraw[:, 0, :], wq).then_inc(s["w_in"], 16)
            act.dma_start(wraw[:, 1, :], wk).then_inc(s["w_in"], 16)
            act.dma_start(wv_sb[:], wv).then_inc(s["w_in"], 16)
            act.dma_start(wmod_sb[:, 2 * C:6 * C], wmod[:, 2 * C:6 * C]).then_inc(s["wmod_in1"], 16)
            act.dma_start(bo8[:], bo.partition_broadcast(B)).then_inc(s["wmod_in1"], 16)
            act.wait_ge(s["cT_ps"], 1)
            nc.scalar.activation(cT[:, 1, :], psM[:, 0:B], ACT.Exp, scale=-1.0).then_inc(s["e_c"], 1)

            def modulate(b):
                act.wait_ge(s["xnT_ps"], b + 1)
                if b == 0:
                    act.wait_ge(s["modT_ok"], 2)
                if b >= 1:
                    act.wait_ge(s["v_ps"], b)
                nc.scalar.activation(hT[:], psM[:, 0:L], ACT.Identity, scale=modT[:, 1, b:b + 1],
                                     bias=modT[:, 0, b:b + 1]).then_inc(s["hT_ready"], 1)

            def qk_copy(b):
                act.wait_ge(s["qk_ps"], b + 1)
                if b == 0:
                    act.wait_ge(s["wqk_ok"], 3)
                if b >= 1:
                    act.wait_ge(s["residuals"], 3 * b)
                nc.scalar.activation(qkf[:, 0, :], psM[:, 0:L], ACT.Identity, bias=bqk[:, 2:3],
                                     scale=float(D) ** -0.5).then_inc(s["qkf_ready"], 1)
                nc.scalar.activation(qkf[:, 1, :], psM[:, L:2 * L], ACT.Identity,
                                     bias=bqk[:, 1:2]).then_inc(s["qkf_ready"], 1)

            def cast_part(b):
                act.wait_ge(s["qkf_ready"], 2 * b + 2)
                if b >= 1:
                    act.wait_ge(s["parts_stored"], 16 * b)
                nc.scalar.copy(parts[:, :, 0, :], qkf[:]).then_inc(s["part_cast"], 1)

            def m_copy(b, half):
                act.wait_ge(s["mT_ps"], 2 * b + half + 1)
                if b >= 2:
                    act.wait_ge(s[f"m_in{half}"], 16 * (b - 1))
                nc.scalar.copy(mT[:, b % 2, half, :], psM[0:8, 0:P].bitcast(BF16)).then_inc(s["mT_ready"], 1)
                if b >= 3:
                    act.wait_ge(s["den_steps"], 3 * (b - 2))
                nc.scalar.activation(emin[:, b % 3, half], negmb[:, b % 2, half], ACT.Exp).then_inc(s["emin_ready"], 1)

            def exps(b, j):
                n = NPAIR * b + j
                if n == 0:
                    act.wait_ge(s["wqk_ok"], 2)
                    act.wait_ge(s["modrow_ps"], 1)
                for kt in range(2):
                    act.wait_ge(s["scoresB"], 2 * n + kt + 1)
                    if n >= PRING and j % 4 == 0:
                        act.wait_ge(s["pv"], 4 * (n // 4 - 1))
                    nc.scalar.activation(probs[:, kt, n % PRING], psB[:, kt, :].rearrange("p (h q) -> p h q", h=H2),
                                         ACT.Exp).then_inc(s["exped"], 1)

            def o_copy(b):
                act.wait_ge(s["pv"], 8 * (b + 1))
                if b >= 1:
                    act.wait_ge(s["oT_ps"], b)
                nc.scalar.copy(oS[:], psO[:]).then_inc(s["o_ready"], 1)

            def aT_copy(b):
                act.wait_ge(s["aT_ps"], b + 1)
                if b >= 1:
                    act.wait_ge(s["op_ps"], b)
                nc.scalar.copy(aT[:], psM[:, 0:L]).then_inc(s["aT_ready"], 1)

            def h2T_copy(b):
                act.wait_ge(s["h2T_ps"], b + 1)
                if b >= 1:
                    act.wait_ge(s["lg_ps"], b)
                nc.scalar.copy(h2T[:], psM[:, 0:L]).then_inc(s["h2T_ready"], 1)

            for step in range(-AHEAD, B + 4):
                has = lambda b: 0 <= b < B
                for j in range(NPAIR):
                    if j == 0 and has(step - 4):
                        h2T_copy(step - 4)
                    if j == 0 and has(step + AHEAD):
                        modulate(step + AHEAD)
                    if j == 2 and has(step - 1):
                        m_copy(step - 1, 1)
                    if j == 3 and has(step + AHEAD):
                        qk_copy(step + AHEAD)
                    if j == 4 and has(step + AHEAD):
                        cast_part(step + AHEAD)
                    if j == 5 and has(step):
                        m_copy(step, 0)
                    if j == 7 and has(step - 2):
                        aT_copy(step - 2)
                    if has(step - 1):
                        exps(step - 1, j)
                    if j == 3 and has(step - 2):
                        o_copy(step - 2)

            act.wait_ge(s["wt_steps"], 1)
            nc.scalar.activation(wts[:, 1, :], wts[:, 0, :], ACT.Exp).then_inc(s["wt_exp"], 1)

            def silu(m, r):
                act.wait_ge(s["g_ps"], m + 1)
                nc.scalar.activation(gate_act[:, r], psG[r], ACT.Silu).then_inc(s["silu_ready"], 1)

            def y_copy(n, r, turn):
                act.wait_ge(s["y_ps"], n + 1)
                if not first(turn):
                    act.wait_ge(scattered[r], 16 * turn)
                nc.scalar.copy(ys[:, r], psY).then_inc(s["y_ready"], 1)

            def w3_copy(n, r):
                e = act.value_load(tile_e[0:1, bass.ds(n, 1)], min_val=0, max_val=E - 1)
                nc.scalar.copy(w3_t[:, r], w3_sb[:, bass.ds(e, 1), :].rearrange("c o i -> c (o i)")).then_inc(s["w3_ready"], 1)

            act.wait_ge(s["te_ready"], 1)
            act.wait_ge(s["moe_w"], 48)
            act.wait_ge(s["lhs_ready"], 2 * NT)
            w3_copy(0, 0)
            w3_copy(1, 1)
            silu(0, 0)

            def three_tiles(it):
                for r in range(TRING):
                    n = it * TRING + r
                    if not first(n):
                        act.wait_ge(s["u_ps"], n)
                    w3_copy(n + 2, (r + 2) % TRING)
                    silu(n + 1, (r + 1) % TRING)
                    y_copy(n, r, it)

            three_tiles(0)
            with act.Fori(1, rounds) as it:
                three_tiles(it)
            act.wait_ge(s["u_ps"], rounds * TRING)
            w3_copy(NTILE - 1, 2)
            for r in range(TRING):
                if r < TRING - 1:
                    silu(rounds * TRING + r + 1, r + 1)
                y_copy(rounds * TRING + r, r, rounds)

            for i in range(4):
                act.wait_ge(s[f"y_in{i}"], 32)
                n = NT // 4
                for j in range(n * i, n * i + n):
                    act.activation(y01[:, 0, j], y01[:, 0, j], ACT.Copy, scale=wts[:, 2, j:j + 1]).then_inc(s["y0_scaled"], 1)

        @block.gpsimd
        def _(pool):
            nc.gpsimd.memset(ident[:], 0.0).then_inc(s["masks"], 1)
            nc.gpsimd.memset(ident_b[:], 0.0).then_inc(s["masks"], 1)
            nc.gpsimd.memset(mask_b[:], 0.0).then_inc(s["masks"], 1)
            nc.gpsimd.memset(npad[:], 0.0).then_inc(s["masks"], 1)
            nc.gpsimd.memset(neghalf[:], -0.5).then_inc(s["masks"], 1)
            pool.wait_ge(s["masks"], 5)
            for t in (ident, ident_b):
                nc.gpsimd.affine_select(out=t[:], in_=t[:], compare_op=ALU.not_equal, fill=1.0, base=0,
                                        pattern=[[-1, P]], channel_multiplier=1).then_inc(s["consts"], 1)
            for qt, sign in ((0, 1), (1, -1)):
                nc.gpsimd.affine_select(out=mask_b[:, qt], in_=mask_b[:, qt], compare_op=ALU.is_ge, fill=MASKED, base=0,
                                        pattern=[[0, H2], [-sign, P]], channel_multiplier=sign).then_inc(s["consts"], 1)
            nc.gpsimd.iota(npad_i[:, 0:1], [[0, 1]], base=P, channel_multiplier=-1).then_inc(s["masks"], 1)
            nc.gpsimd.iota(npad_i[:, 1:2], [[0, 1]], base=1, channel_multiplier=1).then_inc(s["masks"], 1)
            pool.wait_ge(s["masks"], 7)
            nc.gpsimd.tensor_copy(npad[:], npad_i[:]).then_inc(s["consts"], 1)
            nc.gpsimd.memset(vx[:], 0.0).then_inc(s["vx_const"], 1)
            pool.wait_ge(s["vx_const"], 1)
            for par in range(H2):
                nc.gpsimd.memset(vx[:, :, :, :, par, 16 + par:17 + par].rearrange("p r k q o -> p (r k q) o"),
                                 1.0).then_inc(s["vx_const"], 1)

            def ln1_rstd(b):
                pool.wait_ge(s["veps_ok"], b + 1)
                nc.gpsimd.tensor_tensor(rstd[:, 2 * b:2 * b + 2], veps[:, 2 * b:2 * b + 2], neghalf[:, 0:2],
                                        ALU.pow).then_inc(s["rstd_ok"], 1)

            ln1_rstd(0)
            def mask_probs(b, j):
                n = NPAIR * b + j
                v = probs[:, :, n % PRING:n % PRING + 2].rearrange("p k a h q -> p k (a h) q")
                pool.wait_ge(s["exped"], 2 * n + 4)
                for kt, sign in ((0, 1), (1, -1)):
                    u = v[:, kt, :, P:2 * P] if kt == 0 else v[:, kt, :, 0:P]
                    nc.gpsimd.affine_select(out=u, in_=u, compare_op=ALU.is_ge, fill=0.0, base=0,
                                            pattern=[[0, 2 * H2], [-sign, P]], channel_multiplier=sign).then_inc(s["masked"], 1)

            def xg(b):
                for t in range(2):
                    v = x_sb[:, 2 * b + t, :]
                    last = nc.gpsimd.tensor_tensor(v, v, mod_sb[:, b, 4, :], ALU.add)
                last.then_inc(s["xg_ready"], 1)

            def x1_sum(b):
                pool.wait_ge(s["t1_ready"], 2 * b + 2)
                pool.wait_ge(s["xg_ready"], b + 1)
                nc.gpsimd.tensor_tensor(x_sb[:, 2 * b:2 * b + 2, :], t1[:], x_sb[:, 2 * b:2 * b + 2, :],
                                        ALU.add).then_inc(s["x1_ready"], 1)

            def ln2_rstd(b):
                pool.wait_ge(s["ln2_steps"], 3 * b + 3)
                nc.gpsimd.tensor_tensor(rs2[:], ve2[:], neghalf[:, 0:2], ALU.pow).then_inc(s["rs2_ready"], 1)

            def h2_scale(b):
                pool.wait_ge(s["xn2_ready"], 2 * b + 2)
                if b >= 1:
                    pool.wait_ge(s["h2_ready"], b)
                for t in range(2):
                    nc.gpsimd.tensor_tensor(h2m[:, t], xn2[:, t], mod_sb[:, b, 2, :], ALU.mult).then_inc(s["h2m_ready"], 1)

            def h2_shift(b):
                if b >= 2:
                    pool.wait_ge(s[f"h2_stored{b % 2}"], 16 * (b // 2))
                    pool.wait_ge(s["h2T_ps"], b - 1)
                pool.wait_ge(s["h2m_ready"], 2 * b + 2)
                for t in range(2):
                    last = nc.gpsimd.tensor_tensor(h2[:, b % 2, t], h2m[:, t], mod_sb[:, b, 1, :], ALU.add)
                last.then_inc(s["h2_ready"], 1)

            ln1_rstd(1)
            v = iotas[:]
            for lo, n, pattern, base, mult in ((0, P, [[1, P]], 0, 0), (P, 1, [[0, 1]], 0, 1), (P + 1, TOPK * NT, [[1, TOPK * NT]], 1, 0),
                                               (P + 64, NTILE, [[P, NTILE]], (TOPK * NTOK) + P, 1)):
                nc.gpsimd.iota(v[:, lo:lo + n], pattern, base=base, channel_multiplier=mult).then_inc(s["iota_steps"], 1)
            pool.wait_ge(s["iota_steps"], 4)
            for dst, lo, n in ((iota_e, 0, E), (iota_a, 0, NTILE), (iota_c, 0, P), (iota_p, P, 1), (iota_kt, P + 1, TOPK * NT),
                               (dump_row, P + 64, NTILE)):
                nc.gpsimd.tensor_copy(dst[:], v[:, lo:lo + n]).then_inc(s["route_const"], 1)
            nc.gpsimd.memset(ones_b[:], 1.0).then_inc(s["route_const"], 1)
            nc.gpsimd.memset(before[:, 0, :], 0.0).then_inc(s["route_const"], 1)
            nc.gpsimd.memset(upto[:], 0.0).then_inc(s["route_const"], 1)
            pool.wait_ge(s["route_const"], 9)
            nc.gpsimd.affine_select(out=tri[:], in_=ones_b[:], compare_op=ALU.is_gt, fill=0.0, base=0,
                                    pattern=[[1, P]], channel_multiplier=-1).then_inc(s["route_const"], 1)

            for step in range(-AHEAD, B + 4):
                has = lambda b: 0 <= b < B
                for j in range(NPAIR):
                    if j == 3 and has(step - 3):
                        ln2_rstd(step - 3)
                    if j % 2 == 1 and has(step - 1):
                        mask_probs(step - 1, j - 1)
                    if j == 1 and has(step - 3):
                        x1_sum(step - 3)
                    if j == 2 and step > -AHEAD and has(step + AHEAD + 1):
                        ln1_rstd(step + AHEAD + 1)
                    if j == 4 and has(step - 3):
                        h2_scale(step - 3)
                    if j == 5 and has(step - 3):
                        h2_shift(step - 3)
                    if j == 6 and has(step - 1):
                        b = step - 1
                        if b == 0:
                            pool.wait_ge(s["mod_in"], 16)
                        pool.wait_ge(s["xn_ready"], b + 1)
                        xg(b)

            pool.wait_ge(s["idx_ready"], 2)
            for i in range(2):
                pool.wait_ge(s[f"h2_stored{i}"], 16 * (B // 2))

            def table_ready():
                pool.wait_ge(s["idx_ready"], 2)

            def gather(n, r, copied, count):
                table_ready()
                nc.gpsimd.tensor_copy(gidx[r][:], gat_idx[:, bass.ds(n, 1)]).then_inc(s[copied], 1)
                table_ready()
                pool.wait_ge(s[copied], count)
                pool.indirect_dma_start(xs[:, r], None, h2_d, bass.IndirectOffsetOnAxis(ap=gidx[r][:, 0:1], axis=0)).then_inc(gathered[r], 16)

            def scatter(n, r, turn):
                if not first(turn):
                    pool.wait_ge(scattered[r], 16 * turn)
                table_ready()
                nc.gpsimd.tensor_copy(sidx[r][:], sca_idx[:, bass.ds(n, 1)]).then_inc(s["sidx_ready"], 1)
                table_ready()
                pool.wait_ge(s["sidx_ready"], n + 1)
                pool.wait_ge(s["y_ready"], n + 1)
                pool.indirect_dma_start(y_d, bass.IndirectOffsetOnAxis(ap=sidx[r][:, 0:1], axis=0), ys[:, r], None).then_inc(scattered[r], 16)

            for r in range(TRING):
                gather(r, r, "gidx_first", r + 1)

            def three_tiles(it):
                for r in range(TRING):
                    n = it * TRING + r
                    pool.wait_ge(s["xsT_ps"], n + 1)
                    gather(n + TRING, r, "gidx_next", n + 1)
                    scatter(n, r, it)

            three_tiles(0)
            with pool.Fori(1, rounds) as it:
                three_tiles(it)
            for r in range(TRING):
                scatter(rounds * TRING + r, r, rounds)

        @block.vector
        def _(dve):
            def ln1_stats(b):
                if b in (0, 1, 3):
                    dve.wait_ge(s[f"x_in{min(b, 2)}"], 16)
                for i in range(2 * b, 2 * b + 2):
                    last = nc.vector.bn_stats(stats[:, i, :], x_sb[:, i, :])
                last.then_inc(s["ln1_steps"], 1)
                dve.wait_ge(s["ln1_steps"], 2 * b + 1)
                for i in range(2 * b, 2 * b + 2):
                    last = nc.vector.bn_aggr(mv[:, i, :], stats[:, i, :])
                last.then_inc(s["ln1_steps"], 1)
                dve.wait_ge(s["ln1_steps"], 2 * b + 2)
                nc.vector.tensor_scalar(veps[:, 2 * b:2 * b + 2], mv[:, 2 * b:2 * b + 2, 1], EPS, None,
                                        ALU.add).then_inc(s["veps_ok"], 1)

            def normalise(b):
                dve.wait_ge(s["rstd_ok"], b + 1)
                if b >= 2:
                    dve.wait_ge(s["xnT_ps"], b - 1)
                for t in range(2):
                    i = 2 * b + t
                    last = nc.vector.tensor_scalar(xn[:, b % 2, t, :], x_sb[:, i, :], mv[:, i, 0:1], rstd[:, i:i + 1],
                                                   ALU.subtract, ALU.mult)
                last.then_inc(s["xn_ready"], 1)

            nc.vector.memset(kd[:].rearrange("p r h q t -> p (r h q t)"), 0.0).then_inc(s["stack_zero"], 1)
            nc.vector.memset(qs[96:128].rearrange("p r q t -> p (r q t)"), 0.0).then_inc(s["stack_zero"], 1)
            dve.wait_ge(s["stack_zero"], 1)
            dve.wait_ge(s["consts"], 1)
            for h in range(H2):
                v = kd[96:128, :, h].rearrange("p r q t -> p r (q t)")
                nc.vector.tensor_scalar(v, v, ident[96:128, 96 + h:97 + h], None, ALU.add).then_inc(s["stack_zero"], 1)
            ln1_stats(0)
            dve.wait_ge(s["e_c"], 1)
            nc.vector.tensor_scalar(cT[:, 0, :], cT[:, 1, :], 1.0, None, ALU.add).then_inc(s["silu_steps"], 1)
            dve.wait_ge(s["silu_steps"], 1)
            nc.vector.reciprocal(cT[:, 2, :], cT[:, 0, :]).then_inc(s["silu_steps"], 1)
            dve.wait_ge(s["silu_steps"], 2)
            nc.vector.tensor_tensor(cT[:, 3, :], psM[:, 0:B], cT[:, 2, :], ALU.mult).then_inc(s["silu_c"], 1)
            normalise(0)
            dve.wait_ge(s["w_in"], 16 * 8)
            for i in range(2):
                nc.vector.tensor_copy(wqk[:, i, :].rearrange("c (h d p) -> c h d p", h=H2, d=D),
                                      wraw[:, i, :].rearrange("c (p h d) -> c h d p", h=H2, d=D)).then_inc(s["wqk_ok"], 1)
            nc.vector.tensor_scalar(bqk[:, 2:3], bqk[:, 0:1], float(D) ** -0.5, None, ALU.mult).then_inc(s["wqk_ok"], 1)
            dve.wait_ge(s["modT_ps"], 1)
            nc.vector.tensor_copy(modT[:, 0, :], psM[:, 0:B]).then_inc(s["modT_ok"], 1)
            nc.vector.tensor_scalar(modT[:, 1, :], psM[:, B:2 * B], 1.0, None, ALU.add).then_inc(s["modT_ok"], 1)

            def mod_rows():
                ps = psO[0:B].rearrange("b h q -> b (h q)").rearrange("b (r c) -> b r c", c=C)
                dve.wait_ge(s["modrow_ps"], 1)
                nc.vector.tensor_copy(modrow[:, 1, :], ps[:, 1, :]).then_inc(s["mod_steps"], 1)
                nc.vector.tensor_scalar(modrow[:, 2, :], ps[:, 2, :], 1.0, None, ALU.add).then_inc(s["mod_steps"], 1)
                sign, gates, g = modrow[:, 5:7, :], modrow[:, 0:4:3, :], ps[:, 0:4:3, :]
                nc.vector.tensor_scalar(sign, g, 0.0, 2.0, ALU.is_ge, ALU.mult).then_inc(s["mod_steps"], 1)
                dve.wait_ge(s["mod_steps"], 3)
                nc.vector.tensor_scalar(sign, sign, -1.0, None, ALU.add).then_inc(s["mod_steps"], 1)
                dve.wait_ge(s["mod_steps"], 4)
                nc.vector.tensor_tensor(gates, g, sign, ALU.mult).then_inc(s["mod_steps"], 1)
                dve.wait_ge(s["mod_steps"], 5)
                nc.vector.scalar_tensor_tensor(out=gates, in0=gates, scalar=0.25, in1=sign,
                                               op0=ALU.max, op1=ALU.mult).then_inc(s["mod_steps"], 1)
                dve.wait_ge(s["mod_steps"], 6)
                nc.vector.tensor_tensor(modrow[:, 4, :], modrow[:, 0, :], bo8[:], ALU.mult).then_inc(s["mod_steps"], 1)

            def split(b, i):
                if i == 0:
                    dve.wait_ge(s["part_cast"], b + 1)
                    nc.vector.tensor_tensor(resid[:], qkf[:], parts[:, :, 0, :], ALU.subtract).then_inc(s["residuals"], 1)
                    dve.wait_ge(s["residuals"], 3 * b + 1)
                    if b >= 1:
                        dve.wait_ge(s["parts_stored"], 16 * b)
                    nc.vector.tensor_copy(parts[:, :, 1, :], resid[:]).then_inc(s["residuals"], 1)
                else:
                    dve.wait_ge(s["residuals"], 3 * b + 2)
                    nc.vector.tensor_tensor(parts[:, :, 2, :], resid[:], parts[:, :, 1, :], ALU.subtract).then_inc(s["residuals"], 1)

            def values(b):
                dve.wait_ge(s["v_ps"], b + 1)
                if b == 0:
                    dve.wait_ge(s["vx_const"], 3)
                if b >= VRING:
                    dve.wait_ge(s["pv"], 8 * (b - VRING + 1))
                for kt in range(2):
                    for par in range(H2):
                        last = nc.vector.tensor_tensor(
                            vx[:, b % VRING, kt, :, par, D * par:D * par + D],
                            psM[:, kt * C:(kt + 1) * C].rearrange("p (q h d) -> p q h d", h=H2, d=D)[:, :, par, :],
                            bv_sb[:].rearrange("p (q h d) -> p q h d", h=H2, d=D)[:, :, par, :], ALU.add)
                last.then_inc(s["v_ready"], 1)

            def row_max(b, j):
                n = NPAIR * b + j
                dve.wait_ge(s["scoresA"], n + 1)
                if j == 0 and b >= 2:
                    dve.wait_ge(s["half_max"], 2 * (b - 1))
                nc.vector.tensor_reduce(negm[:, b % 2, :, :, j],
                                        psA[:, n % 2].rearrange("p q (h k) -> p q h k", h=H2),
                                        AX.X, ALU.max, negate=True).then_inc(s["rowmax"], 1)

            def half_max(b, half):
                dve.wait_ge(s["rowmax"], NPAIR * b + 4 * half + 4)
                if b >= 2:
                    dve.wait_ge(s["mT_ps"], 2 * (b - 2) + half + 1)
                    dve.wait_ge(s["emin_ready"], 2 * (b - 2) + half + 1)
                for qt in range(2):
                    last = nc.vector.tensor_scalar(negmb[:, b % 2, half, qt], negm[:, b % 2, qt, :, 4 * half:4 * half + 4],
                                                   0.0, None, ALU.min)
                last.then_inc(s["half_max"], 1)

            def pad_term(b):
                dve.wait_ge(s["emin_ready"], 2 * b + 2)
                if b == 0:
                    dve.wait_ge(s["consts"], 5)
                for qt in range(2):
                    last = nc.vector.tensor_scalar(
                        den[:, 0, qt, :].rearrange("p (f q h) -> p f h q", f=2, h=H2),
                        emin[:, b % 3, :, qt], npad[:, qt:qt + 1], None, ALU.mult)
                last.then_inc(s["den_steps"], 1)

            def normalise_attn(b):
                dve.wait_ge(s["den_steps"], 3 * b + 1)
                dve.wait_ge(s["oT_ps"], b + 1)
                for qt in range(2):
                    ps = psM[:, qt * 256:(qt + 1) * 256].rearrange("p (q r) -> p q r", r=VCOL)
                    last = nc.vector.tensor_tensor(
                        den[:, 1, qt, :].rearrange("p (q h) -> p q h", h=H2), ps[:, :, 16:18],
                        den[:, 0, qt, :].rearrange("p (q h) -> p q h", h=H2), ALU.add)
                last.then_inc(s["den_steps"], 1)
                dve.wait_ge(s["den_steps"], 3 * b + 2)
                nc.vector.reciprocal(den[:, 2], den[:, 1]).then_inc(s["den_steps"], 1)
                dve.wait_ge(s["den_steps"], 3 * b + 3)
                if b >= 1:
                    dve.wait_ge(s["aT_ps"], b)
                for qt in range(2):
                    ps = psM[:, qt * 256:(qt + 1) * 256].rearrange("p (q r) -> p q r", r=VCOL)[:, :, 0:16]
                    last = nc.vector.tensor_tensor(
                        attn[:, qt, :].rearrange("p (q h d) -> p q h d", h=H2, d=D),
                        ps.rearrange("p q (h d) -> p q h d", d=D),
                        den[:, 2, qt, :].rearrange("p (q h o) -> p q h o", h=H2, o=1).broadcast_to([P, NPAIR, H2, D]),
                        ALU.mult)
                last.then_inc(s["normed"], 1)

            def gate_attn(b):
                dve.wait_ge(s["op_ps"], b + 1)
                if b >= 1:
                    dve.wait_ge(s["x1_ready"], b)
                for t in range(2):
                    nc.vector.tensor_tensor(t1[:, t], psM[:, t * C:(t + 1) * C], mod_sb[:, b, 0, :],
                                            ALU.mult).then_inc(s["t1_ready"], 1)

            def ln2_stats(b):
                dve.wait_ge(s["x1_ready"], b + 1)
                for t in range(2):
                    last = nc.vector.bn_stats(stats2[:, t, :], x_sb[:, 2 * b + t, :])
                last.then_inc(s["ln2_steps"], 1)
                dve.wait_ge(s["ln2_steps"], 3 * b + 1)
                for t in range(2):
                    last = nc.vector.bn_aggr(mv2[:, t, :], stats2[:, t, :])
                last.then_inc(s["ln2_steps"], 1)
                dve.wait_ge(s["ln2_steps"], 3 * b + 2)
                if b >= 1:
                    dve.wait_ge(s["rs2_ready"], b)
                nc.vector.tensor_scalar(ve2[:], mv2[:, :, 1], EPS, None, ALU.add).then_inc(s["ln2_steps"], 1)

            def ln2_normalise(b):
                dve.wait_ge(s["rs2_ready"], b + 1)
                if b >= 1:
                    dve.wait_ge(s["h2m_ready"], 2 * b)
                for t in range(2):
                    nc.vector.tensor_scalar(xn2[:, t], x_sb[:, 2 * b + t, :], mv2[:, t, 0:1], rs2[:, t:t + 1],
                                            ALU.subtract, ALU.mult).then_inc(s["xn2_ready"], 1)

            def top2(b):
                dve.wait_ge(s["lg_ps"], b + 1)
                nc.vector.tensor_copy(lg[:, 2 * b:2 * b + 2, :],
                                      psM[:, 0:16].rearrange("p (t e) -> p t e", e=8)).then_inc(s["lg_ready"], 1)
                dve.wait_ge(s["lg_ready"], b + 1)
                for t in range(2 * b, 2 * b + 2):
                    last = nc.vector.max(top[:, t, :], lg[:, t, :])
                    last.then_inc(s["top_ready"], 1)
                dve.wait_ge(s["top_ready"], 4 * b + 2)
                for t in range(2 * b, 2 * b + 2):
                    nc.vector.max_index(topi[:, t, :], top[:, t, :], lg[:, t, :]).then_inc(s["top_ready"], 1)
                dve.wait_ge(s["top_ready"], 4 * b + 4)
                tt = slice(2 * b, 2 * b + 2)
                nc.vector.tensor_copy(topf[:, tt], topi[:, tt, 0:TOPK]).then_inc(s["picks_ready"], 1)
                dve.wait_ge(s["picks_ready"], 6 * b + 1)
                if b == 0:
                    dve.wait_ge(s["route_const"], 10)
                for k in range(TOPK):
                    nc.vector.tensor_tensor(pick[:, k, tt], iota_e[:].rearrange("p (o e) -> p o e", o=1).broadcast_to([P, 2, E]),
                                            topf[:, tt, k:k + 1].broadcast_to([P, 2, E]), ALU.is_equal).then_inc(s["picks_ready"], 1)
                dve.wait_ge(s["picks_ready"], 6 * b + 3)
                nc.vector.tensor_tensor(used[:, tt], pick[:, 0, tt], pick[:, 1, tt], ALU.add).then_inc(s["picks_ready"], 1)
                dve.wait_ge(s["picks_ready"], 6 * b + 4)
                for i in range(2):
                    nc.vector.tensor_tensor(before[:, 2 * b + i + 1], before[:, 2 * b + i], used[:, 2 * b + i],
                                            ALU.add).then_inc(s["picks_ready"], 1)
                    dve.wait_ge(s["picks_ready"], 6 * b + 5 + i)

            for step in range(-AHEAD, B + 4):
                if step == 1:
                    mod_rows()
                has = lambda b: 0 <= b < B
                for j in range(NPAIR):
                    if j == 1 and has(step - 3):
                        gate_attn(step - 3)
                    if j == 2 and has(step - 4):
                        top2(step - 4)
                    if j == 3 and has(step - 3):
                        ln2_stats(step - 3)
                    if j == 4 and has(step + AHEAD):
                        values(step + AHEAD)
                    if j == 6 and has(step - 2):
                        normalise_attn(step - 2)
                    if has(step):
                        row_max(step, j)
                    if j == 0 and has(step - 1):
                        half_max(step - 1, 1)
                    if j == 1 and has(step + AHEAD + 1):
                        ln1_stats(step + AHEAD + 1)
                    if j == 3 and has(step):
                        half_max(step, 0)
                    if j == 4 and has(step - 3):
                        ln2_normalise(step - 3)
                    if j == 4 and has(step - 2):
                        pad_term(step - 2)
                    if j == 5 and has(step + AHEAD):
                        split(step + AHEAD, 0)
                    if j == 6 and has(step + AHEAD):
                        split(step + AHEAD, 1)
                    if j == 7 and has(step + AHEAD + 1):
                        normalise(step + AHEAD + 1)

            count = [0]

            def step_done(ins):
                count[0] += 1
                ins.then_inc(s["pos_steps"], 1)
                dve.wait_ge(s["pos_steps"], count[0])

            nc.vector.tensor_tensor(wts[:, 0, :], top[:, :, 1], top[:, :, 0], ALU.subtract).then_inc(s["wt_steps"], 1)
            dve.wait_ge(s["rank_ps"], 1)
            step_done(nc.vector.tensor_scalar(ntile_e[:, 0], psR[:, NT * E:(NT + 1) * E], P / 2 - 0.5, 1.0 / P, ALU.add, ALU.mult))
            step_done(nc.vector.tensor_scalar(ntile_e[:, 1], ntile_e[:, 0], ROUND, None, ALU.add))
            step_done(nc.vector.tensor_scalar(upto[:, 0, E:], ntile_e[:, 1], -ROUND, None, ALU.add))
            for i in range(3):
                d = 1 << i
                step_done(nc.vector.tensor_tensor(upto[:, i + 1, E:], upto[:, i, E:], upto[:, i, E - d:2 * E - d], ALU.add))
            step_done(nc.vector.scalar_tensor_tensor(
                out=place[:], in0=upto[:, 3:4, E - 1:2 * E - 1].broadcast_to([P, NT, E]), scalar=float(P),
                in1=psR[:, 0:NT * E].rearrange("p (t e) -> p t e", e=E), op0=ALU.mult, op1=ALU.add))
            for k in range(TOPK):
                last = nc.vector.tensor_tensor(picked[:, k], pick[:, k], place[:], ALU.mult)
            step_done(last)
            step_done(nc.vector.tensor_reduce(pos[:, 0].rearrange("p (k t) -> p k t", k=TOPK), picked[:], AX.X, ALU.add))
            step_done(nc.vector.tensor_scalar(pos[:, 1], pos[:, 0], 0.5 - P / 2, 1.0 / P, ALU.add, ALU.mult))
            step_done(nc.vector.tensor_scalar(pos[:, 2], pos[:, 1], ROUND, None, ALU.add))
            step_done(nc.vector.tensor_scalar(pos[:, 3], pos[:, 2], -ROUND, None, ALU.add))
            step_done(nc.vector.scalar_tensor_tensor(out=pos[:, 4], in0=pos[:, 3], scalar=-float(P), in1=pos[:, 0],
                                                     op0=ALU.mult, op1=ALU.add))
            nkt = TOPK * NT
            step_done(nc.vector.tensor_tensor(
                inv_sel[:], iota_a[:].rearrange("p (o a) -> p o a", o=1).broadcast_to([P, nkt, NTILE]),
                pos[:, 3].rearrange("p (k o) -> p k o", o=1).broadcast_to([P, nkt, NTILE]), ALU.is_equal))
            nc.vector.tensor_scalar(inv_rhs[:, 0], inv_sel[:], iota_p[:, 0:1], None, ALU.mult)
            step_done(nc.vector.tensor_tensor(
                inv_rhs[:, 1], inv_sel[:], iota_kt[:].rearrange("p (k o) -> p k o", o=1).broadcast_to([P, nkt, NTILE]), ALU.mult))
            for i in range(nkt):
                if i >= 4:
                    dve.wait_ge(s["lhs_used"], i - 3)
                nc.vector.tensor_scalar(inv_lhs[:, i % 4], iota_c[:], pos[:, 4, i:i + 1], None, ALU.is_equal).then_inc(s["lhs_ready"], 1)
            dve.wait_ge(s["inv_ps"], 1)
            row, kt = psM[:, 0:NTILE], psM[:, NTILE:2 * NTILE]
            step_done(nc.vector.tensor_copy(inv[:, 4], kt))
            step_done(nc.vector.scalar_tensor_tensor(out=inv[:, 0], in0=inv[:, 4], scalar=float(P), in1=row, op0=ALU.mult, op1=ALU.add))
            nc.vector.tensor_scalar(inv[:, 1], inv[:, 4], NT + 0.5, -float(NTOK), ALU.is_ge, ALU.mult)
            step_done(nc.vector.scalar_tensor_tensor(out=inv[:, 2], in0=inv[:, 4], scalar=0.5, in1=dump_row[:], op0=ALU.is_lt, op1=ALU.mult))
            step_done(nc.vector.scalar_tensor_tensor(out=inv[:, 3], in0=inv[:, 0], scalar=-float(P), in1=inv[:, 1], op0=ALU.add, op1=ALU.add))
            nc.vector.tensor_scalar(gat_idx[:], inv[:, 3], 0.0, None, ALU.max).then_inc(s["idx_ready"], 1)
            nc.vector.scalar_tensor_tensor(out=sca_idx[:], in0=inv[:, 0], scalar=-float(P), in1=inv[:, 2],
                                           op0=ALU.add, op1=ALU.add).then_inc(s["idx_ready"], 1)

            step_done(nc.vector.tensor_tensor(
                te_cmp[:], upto[0:1, 3:4, E:].broadcast_to([1, NTILE, E]),
                iota_a[0:1].rearrange("p (a o) -> p a o", o=1).broadcast_to([1, NTILE, E]), ALU.is_le))
            step_done(nc.vector.tensor_reduce(te_sum[:], te_cmp[:], AX.X, ALU.add))
            nc.vector.tensor_scalar(tile_e[:], te_sum[:], float(E - 1), None, ALU.min).then_inc(s["te_ready"], 1)
            dve.wait_ge(s["wt_exp"], 1)
            step_done(nc.vector.tensor_scalar(wts[:, 3, :], wts[:, 1, :], 1.0, None, ALU.add))
            step_done(nc.vector.reciprocal(wts[:, 2, :], wts[:, 3, :]))
            step_done(nc.vector.tensor_tensor(wts[:, 3, :], wts[:, 1, :], wts[:, 2, :], ALU.mult))
            def xsT_copy(n, r):
                dve.wait_ge(s["xsT_ps"], n + 1)
                nc.vector.tensor_copy(xsT[:, r], psX).then_inc(s["xsT_ready"], 1)

            def gate_hidden(m, r):
                dve.wait_ge(s["silu_ready"], m + 1)
                dve.wait_ge(s["u_ps"], m + 1)
                nc.vector.tensor_tensor(hid[:, r], psU[r], gate_act[:, r], ALU.mult).then_inc(s["hid_ready"], 1)

            def expert(n):
                return dve.value_load(tile_e[0:1, bass.ds(n, 1)], min_val=0, max_val=E - 1)

            def w1_copy(n, r, e):
                nc.vector.tensor_copy(w1_t[:, r], w1_sb[:, bass.ds(e, 1), :].rearrange("c o i -> c (o i)")).then_inc(s["w1_ready"], 1)

            def w2_copy(n, r, e):
                nc.vector.tensor_copy(w2_t[:, r], w2_sb[:, bass.ds(e, 1)].rearrange("p o k c -> p (o k c)")).then_inc(s["w2_ready"], 1)

            dve.wait_ge(s["moe_w"], 48)
            for r in range(2):
                w1_copy(r, r, expert(r))
                xsT_copy(r, r)
            for r in range(2):
                w2_copy(r, r, expert(r))
            gate_hidden(0, 0)

            def three_tiles(it):
                for r in range(TRING):
                    n = it * TRING + r
                    e = expert(n + 2)
                    if not first(n):
                        dve.wait_ge(s["u_ps"], n)
                    w1_copy(n + 2, (r + 2) % TRING, e)
                    xsT_copy(n + 2, (r + 2) % TRING)
                    gate_hidden(n + 1, (r + 1) % TRING)
                    w2_copy(n + 2, (r + 2) % TRING, e)

            three_tiles(0)
            with dve.Fori(1, rounds) as it:
                three_tiles(it)
            e = expert(NTILE - 1)
            dve.wait_ge(s["u_ps"], rounds * TRING)
            w1_copy(NTILE - 1, 2, e)
            xsT_copy(NTILE - 1, 2)
            gate_hidden(NTILE - 2, 1)
            w2_copy(NTILE - 1, 2, e)
            gate_hidden(NTILE - 1, 2)

            n = NT // 4
            base = count[0]
            for i in range(4):
                tt = slice(n * i, n * i + n)
                bb = slice(n * i // 2, n * (i + 1) // 2)
                dve.wait_ge(s[f"y_in{i}"], 32)
                step_done(nc.vector.tensor_tensor(comb[:, tt], y01[:, 1, tt], wts[:, 3, tt].rearrange("p (t o) -> p t o", o=1).broadcast_to([P, n, C]), ALU.mult))
                dve.wait_ge(s["y0_scaled"], n * (i + 1))
                step_done(nc.vector.tensor_tensor(comb[:, tt], comb[:, tt], y01[:, 0, tt], ALU.add))
                v = comb[:, tt].rearrange("p (b t) c -> p b t c", t=2)
                step_done(nc.vector.tensor_tensor(v, v, mod_sb[:, bb, 3:4, :].broadcast_to([P, n // 2, 2, C]), ALU.mult))
                nc.vector.tensor_tensor(outb[:, tt], comb[:, tt], x_sb[:, tt], ALU.add).then_inc(s["out_ready"], 1)

        @block.tensor
        def _(pe):
            last_psM = [None]

            def take_psM(release, value):
                if last_psM[0]:
                    pe.wait_ge(*last_psM[0])
                last_psM[0] = (s[release], value)

            pe.wait_ge(s["consts"], 2)
            pe.wait_ge(s["c_in"], 16)
            nc.tensor.transpose(psM[:, 0:B], c_sb[:], ident[0:B, 0:B]).then_inc(s["cT_ps"], 1)
            pe.wait_ge(s["silu_c"], 1)
            pe.wait_ge(s["wmod_in0"], 16)
            for i in range(2):
                last = nc.tensor.matmul(psM[:, i * B:(i + 1) * B], wmod_sb[:, i * C:(i + 1) * C], cT[:, 3, :],
                                        start=True, stop=True)
            last.then_inc(s["modT_ps"], 1)
            take_psM("modT_ok", 2)

            def mod_matmul():
                pe.wait_ge(s["wmod_in1"], 32)
                nc.tensor.matmul(psO[0:B].rearrange("b h q -> b (h q)"), cT[:, 3, :], wmod_sb[:, 2 * C:6 * C],
                                 start=True, stop=True).then_inc(s["modrow_ps"], 1)

            def xn_T(b):
                pe.wait_ge(s["xn_ready"], b + 1)
                take_psM("hT_ready", b + 1)
                for t in range(2):
                    last = nc.tensor.transpose(psM[:, t * P:(t + 1) * P], xn[:, b % 2, t, :], ident[:])
                last.then_inc(s["xnT_ps"], 1)

            def project_qk(b):
                if b == 0:
                    pe.wait_ge(s["wqk_ok"], 2)
                take_psM("qkf_ready", 2 * b + 2)
                for i in range(2):
                    last = nc.tensor.matmul(psM[:, i * L:(i + 1) * L], wqk[:, i, :], hT[:], start=True, stop=True)
                last.then_inc(s["qk_ps"], 1)

            def project_v(b):
                take_psM("v_ready", b + 1)
                for t in range(2):
                    last = nc.tensor.matmul(psM[:, t * C:(t + 1) * C], hT[:, t * P:(t + 1) * P], wv_sb[:], start=True, stop=True)
                last.then_inc(s["v_ps"], 1)

            def scores_A(b, j):
                n = NPAIR * b + j
                if j == 0:
                    pe.wait_ge(stack_in[b % RING], 16 * NLOADS * (b // RING + 1))
                if n >= 2:
                    pe.wait_ge(s["rowmax"], n - 1)
                r = b % RING
                for qt in range(2):
                    nc.tensor.matmul(psA[:, n % 2, qt, :].rearrange("p (h k) -> p h k", h=H2),
                                     qs[0:SROWS, r, j, qt * P:(qt + 1) * P], kd[0:SROWS, r, :, j, :], start=True, stop=False)
                    off = (1 - qt) * P
                    last = nc.tensor.matmul(psA[:, n % 2, qt, :].rearrange("p (h k) -> p h k", h=H2)[:, :, off:off + P],
                                            ident_b[:], mask_b[:, qt], start=False, stop=True)
                last.then_inc(s["scoresA"], 1)

            def max_T(b, half):
                pe.wait_ge(s["half_max"], 2 * b + half + 1)
                take_psM("mT_ready", 2 * b + half + 1)
                pb = psM[0:8, 0:P].bitcast(BF16)
                for qt in range(2):
                    last = nc.tensor.transpose(pb[:, qt * P:(qt + 1) * P],
                                               negmb[:, b % 2, half, qt].rearrange("p h q -> p (h q)"), ident_b[:])
                last.then_inc(s["mT_ps"], 1)

            def scores_B(b, j):
                n = NPAIR * b + j
                r = b % RING
                if j % 4 == 0:
                    pe.wait_ge(s[f"m_in{j // 4}"], 16 * (b + 1))
                for kt in range(2):
                    if n >= 1:
                        pe.wait_ge(s["exped"], 2 * n + kt - 1)
                    for h in range(H2):
                        last = nc.tensor.matmul(psB[:, kt, h * L:(h + 1) * L], kd[:, r, h, j, kt * P:(kt + 1) * P],
                                                qs[:, r, j, :], start=True, stop=True)
                    last.then_inc(s["scoresB"], 1)

            def weigh_values(b, i):
                half, piece = i // 4, i % 4
                h, kt = piece // 2, piece % 2
                if piece == 0:
                    pe.wait_ge(s["masked"], 8 * b + 4 * half + 4)
                    if half == 0:
                        pe.wait_ge(s["v_ready"], b + 1)
                    if half == 0 and b >= 1:
                        pe.wait_ge(s["o_ready"], b)
                    if half == 0 and b == 0:
                        pe.wait_ge(s["mod_steps"], 5)
                for g in range(4):
                    j = 4 * half + g
                    last = nc.tensor.matmul(psO[32 * g:32 * g + 32, half, :], vx[:, b % VRING, kt, j, h, :],
                                            probs[:, kt, j, h, :], start=(piece == 0), stop=(piece == 3))
                last.then_inc(s["pv"], 1)

            def o_T(b):
                pe.wait_ge(s["o_ready"], b + 1)
                take_psM("normed", b + 1)
                for qt in range(2):
                    for half in range(2):
                        i = 2 * qt + half
                        last = nc.tensor.transpose(psM[:, i * P:(i + 1) * P], oS[:, half, qt * P:(qt + 1) * P], ident[:])
                last.then_inc(s["oT_ps"], 1)

            def attn_T(b):
                take_psM("aT_ready", b + 1)
                for t in range(2):
                    last = nc.tensor.transpose(psM[:, t * P:(t + 1) * P], attn[:, t, :], ident[:])
                last.then_inc(s["aT_ps"], 1)

            def project_out(b):
                if b == 0:
                    pe.wait_ge(s["wo_in"], 32)
                take_psM("t1_ready", 2 * b + 2)
                for t in range(2):
                    last = nc.tensor.matmul(psM[:, t * C:(t + 1) * C], aT[:, t * P:(t + 1) * P], wo_sb[:], start=True, stop=True)
                last.then_inc(s["op_ps"], 1)

            def h2_T(b):
                pe.wait_ge(s["h2_ready"], b + 1)
                take_psM("h2T_ready", b + 1)
                for t in range(2):
                    last = nc.tensor.transpose(psM[:, t * P:(t + 1) * P], h2[:, b % 2, t, :], ident[:])
                last.then_inc(s["h2T_ps"], 1)

            def logits(b):
                take_psM("lg_ready", b + 1)
                for t in range(2):
                    last = nc.tensor.matmul(psM[:, 8 * t:8 * t + 8], h2T[:, t * P:(t + 1) * P], gate_sb[:], start=True, stop=True)
                last.then_inc(s["lg_ps"], 1)

            for step in range(-AHEAD, B + 4):
                if step == 0:
                    mod_matmul()
                a, nxt, prev = step, step + AHEAD, step - 1
                has = lambda b: 0 <= b < B
                for j in range(NPAIR):
                    if j == 0 and has(nxt):
                        xn_T(nxt)
                    if j == 1 and has(step - 4):
                        logits(step - 4)
                    if j == 7 and has(step - 2):
                        attn_T(step - 2)
                    if has(a):
                        scores_A(a, j)
                    if j == 0 and has(step - 3):
                        project_out(step - 3)
                    if j == 1 and has(prev):
                        max_T(prev, 1)
                    if j == 2 and has(nxt):
                        project_qk(nxt)
                    if j == 3 and has(nxt):
                        project_v(nxt)
                    if j == 4 and has(a):
                        max_T(a, 0)
                    if j == 5 and has(step - 2):
                        o_T(step - 2)
                    if j == 7 and has(step - 3):
                        h2_T(step - 3)
                    if has(prev):
                        scores_B(prev, j)
                    for i in {5: (0,), 6: (1,), 7: (2, 3)}.get(j, ()):
                        if has(prev):
                            weigh_values(prev, i)
                    for i in {1: (4,), 2: (5,), 3: (6, 7)}.get(j, ()):
                        if has(prev - 1):
                            weigh_values(prev - 1, i)

            pe.wait_ge(s["picks_ready"], 6 * B)
            rank = psR[:, 0:NT * E]
            pe.wait_ge(s["exped"], 2 * NPAIR * B)
            nc.tensor.matmul(rank, tri[:], used[:].rearrange("p t e -> p (t e)"), start=True, stop=False)
            nc.tensor.matmul(rank, ones_b[:], before[:, 0:NT].rearrange("p t e -> p (t e)"), start=False, stop=True)
            nc.tensor.matmul(psR[:, NT * E:(NT + 1) * E], ones_b[:], before[:, NT], start=True, stop=True).then_inc(s["rank_ps"], 1)
            pe.wait_ge(*last_psM[0])
            nkt = TOPK * NT
            for i in range(nkt):
                pe.wait_ge(s["lhs_ready"], i + 1)
                last = nc.tensor.matmul(psM[:, 0:2 * NTILE].rearrange("p (w a) -> p w a", w=2), inv_lhs[:, i % 4],
                                        inv_rhs[:, :, i, :], start=(i == 0), stop=(i == nkt - 1))
                last.then_inc(s["lhs_used"], 1) if i < nkt - 1 else last.then_inc(s["inv_ps"], 1)

            pe.wait_ge(s["moe_w"], 48)
            pe.wait_ge(s["te_ready"], 1)
            pe.wait_ge(s["idx_ready"], 2)

            def xs_T(n, r, turn):
                pe.wait_ge(gathered[r], 16 * (turn + 1))
                if not first(n):
                    pe.wait_ge(s["xsT_ready"], n)
                nc.tensor.transpose(psX, xs[:, r], ident[:]).then_inc(s["xsT_ps"], 1)

            def up(m, r):
                pe.wait_ge(s["xsT_ready"], m + 1)
                for ps, w, here, done in ((psG[r], w1_t, "w1_ready", "g_ps"), (psU[r], w3_t, "w3_ready", "u_ps")):
                    pe.wait_ge(s[here], m + 1)
                    for k in range(NC):
                        last = nc.tensor.matmul(ps[:, k * P:(k + 1) * P], w[:, r, k * P:(k + 1) * P],
                                                xsT[:, r], start=True, stop=True)
                    last.then_inc(s[done], 1)

            def down(n, r):
                pe.wait_ge(s["hid_ready"], n + 1)
                pe.wait_ge(s["w2_ready"], n + 1)
                if not first(n):
                    pe.wait_ge(s["y_ready"], n)
                for k in range(NC):
                    last = nc.tensor.matmul(psY, hid[:, r, k * P:(k + 1) * P], w2_t[:, r, k * C:(k + 1) * C],
                                            start=(k == 0), stop=(k == NC - 1))
                last.then_inc(s["y_ps"], 1)

            xs_T(0, 0, 0)
            xs_T(1, 1, 0)
            up(0, 0)

            def three_tiles(it):
                for r in range(TRING):
                    n = it * TRING + r
                    up(n + 1, (r + 1) % TRING)
                    xs_T(n + 2, (r + 2) % TRING, it + (r + 2) // TRING)
                    down(n, r)

            three_tiles(0)
            with pe.Fori(1, rounds) as it:
                three_tiles(it)
            for r in range(TRING):
                n = rounds * TRING + r
                if r < TRING - 1:
                    up(n + 1, r + 1)
                if r < TRING - 2:
                    xs_T(n + 2, r + 2, rounds)
                down(n, r)


_INS = ("L0_attn_x", "L0_attn_wq", "L0_attn_bq", "L0_attn_wk", "L0_attn_bk", "L0_attn_wv", "L0_attn_bv", "L0_attn_wo", "L0_attn_bo",
        "L0_ffn_gate", "L0_ffn_experts_w1", "L0_ffn_experts_w2", "L0_ffn_experts_w3", "L0_c", "L0_wmod")


def kernel(**inputs):
    import numpy as _np
    import concourse.bacc as _bacc
    from concourse import mybir as _mybir
    from concourse.bass_utils import run_bass_kernel_spmd as _run

    nc = _bacc.Bacc("TRN2", target_bir_lowering=False, num_devices=1)
    arrays, args = {}, []
    for name in _INS:
        a = _np.ascontiguousarray(inputs[name])
        arrays[f"in_{name}_dram"] = a
        args.append(nc.dram_tensor(f"in_{name}_dram", a.shape, _mybir.dt.from_np(a.dtype), kind="ExternalInput").ap())
    shape = inputs["L0_attn_x"].shape
    out = nc.dram_tensor("out_0_dram", shape, _mybir.dt.float32, kind="ExternalOutput").ap()
    adaln_attention_moe(nc, *args, out)
    r = _run(nc, [arrays], core_ids=[0])
    return r.results[0]["out_0_dram"]
```

```python
from contextlib import ExitStack

import numpy as np

import concourse.bass as bass
from concourse import mybir

P = 128
ALU = mybir.AluOpType
ACT = mybir.ActivationFunctionType
AX = mybir.AxisListType
F32 = mybir.dt.float32
BF16 = mybir.dt.bfloat16
I32 = mybir.dt.int32
U32 = mybir.dt.uint32

H2 = 2
D = 8
NPAIR = 8
QP = (0, 0, 0, 1, 1, 2)
KP = (0, 1, 2, 0, 1, 0)
NSLOT = len(QP)
HROWS = NSLOT * D
SROWS = H2 * HROWS
RING = 3
VRING = 4
AHEAD = 2
VCOL = 32
PRING = 8
MASKED = -1e30
EPS = 1e-5


def first(v):
    return isinstance(v, int) and v == 0


def adaln_attention_moe(nc, x, wq, bq, wk, bk, wv, bv, wo, bo, gate, w1, w2, w3, c, wmod, out):
    B, L, C = x.shape
    NT = B * L // P
    E, _, I = w1.shape
    NC = I // P
    NTOK = B * L
    TOPK = 2
    NTILE = (TOPK * NTOK - E) // P + E
    TRING = 3
    ROUND = 1.5 * 2.0 ** 23
    assert L == 2 * P and C == P and NTILE % TRING == 0

    with ExitStack() as ctx:
        def sb(name, shape, dt=F32):
            return ctx.enter_context(nc.sbuf_tensor(name, shape, dt))

        def sem(name):
            return ctx.enter_context(nc.semaphore(name))

        parts_d = nc.dram_tensor("parts_d", [B, 2, 3, P, L], BF16, kind="Internal").ap()
        mod_d = nc.dram_tensor("mod_d", [B, 5 * P], F32, kind="Internal").ap()
        h2_d = nc.dram_tensor("h2_d", [B * L, C], F32, kind="Internal").ap()

        y_d = nc.dram_tensor("y_d", [TOPK * NTOK + NTILE * P, C], F32, kind="Internal").ap()

        w1_sb = sb("w1_sb", [P, E, I])
        w3_sb = sb("w3_sb", [P, E, I])
        w2_sb = sb("w2_sb", [P, E, NC, C])
        tri = sb("tri", [P, P], BF16)
        ones_b = sb("ones_b", [P, P], BF16)
        iota_e = sb("iota_e", [P, E])
        iota_a = sb("iota_a", [P, NTILE])
        iota_c = sb("iota_c", [P, P], BF16)
        iota_p = sb("iota_p", [P, 1])
        iota_kt = sb("iota_kt", [P, TOPK * NT])
        dump_row = sb("dump_row", [P, NTILE])
        iotas = sb("iotas", [P, 256], I32)
        topf = sb("topf", [P, NT, TOPK])
        pick = sb("pick", [P, TOPK, NT, E], BF16)
        used = sb("used", [P, NT, E], BF16)
        before = sb("before", [P, NT + 1, E], BF16)
        ntile_e = sb("ntile_e", [P, 3, E])
        upto = sb("upto", [P, 4, 2 * E])
        gat_idx = sb("gat_idx", [P, NTILE], I32)
        sca_idx = sb("sca_idx", [P, NTILE], I32)
        te_cmp = sb("te_cmp", [1, NTILE, E])
        te_sum = sb("te_sum", [1, NTILE])
        tile_e = sb("tile_e", [1, NTILE], I32)
        wts = sb("wts", [P, 4, NT])
        gidx = [sb(f"gidx{r}", [P, 1], I32) for r in range(TRING)]
        sidx = [sb(f"sidx{r}", [P, 1], I32) for r in range(TRING)]
        x_sb = sb("x_sb", [P, NT, C])
        mod_sb = sb("mod_sb", [P, B, 5, C])
        ident = sb("ident", [P, P])
        ident_b = sb("ident_b", [P, P], BF16)
        mask_b = sb("mask_b", [P, 2, H2, P], BF16)
        c_sb = sb("c_sb", [B, C])
        cT = sb("cT", [P, 4, B])
        modrow = sb("modrow", [B, 7, C])
        bo8 = sb("bo8", [B, C])
        modT = sb("modT", [P, 2, B])
        wqk = sb("wqk", [P, 2, C])
        wv_sb = sb("wv_sb", [P, C])
        wo_sb = sb("wo_sb", [P, C])
        gate_sb = sb("gate_sb", [P, 8])
        bqk = sb("bqk", [P, 4])
        bv_sb = sb("bv_sb", [P, C])
        stats = sb("stats", [P, NT, 6])
        mv = sb("mv", [P, NT, 2])
        veps = sb("veps", [P, NT])
        rstd = sb("rstd", [P, NT])
        neghalf = sb("neghalf", [P, NT])
        xn = sb("xn", [P, 2, 2, C])
        hT = sb("hT", [P, L])
        qkf = sb("qkf", [P, 2, L])
        parts = sb("parts", [P, 2, 3, L], BF16)
        resid = sb("resid", [P, 2, L])
        qs = sb("qs", [P, RING, NPAIR, L], BF16)
        kd = sb("kd", [P, RING, H2, NPAIR, L], BF16)
        vx = sb("vx", [P, VRING, 2, NPAIR, H2, VCOL])
        negm = sb("negm", [P, 2, 2, H2, NPAIR])
        negmb = sb("negmb", [P, 2, 2, 2, H2, 4], BF16)
        mT = sb("mT", [8, 2, 2, L], BF16)
        emin = sb("emin", [P, 3, 2, 2, H2, 4])
        npad_i = sb("npad_i", [P, 2], I32)
        npad = sb("npad", [P, 2])
        probs = sb("probs", [P, 2, PRING, H2, L])
        oS = sb("oS", [P, 2, L])
        den = sb("den", [P, 3, 2, H2 * NPAIR])
        attn = sb("attn", [P, 2, C])
        aT = sb("aT", [P, L])
        t1 = sb("t1", [P, 2, C])
        stats2 = sb("stats2", [P, 2, 6])
        mv2 = sb("mv2", [P, 2, 2])
        ve2 = sb("ve2", [P, 2])
        rs2 = sb("rs2", [P, 2])
        xn2 = sb("xn2", [P, 2, C])
        h2m = sb("h2m", [P, 2, C])
        h2 = sb("h2", [P, 2, 2, C])
        h2T = sb("h2T", [P, L])
        lg = sb("lg", [P, NT, 8])
        top = sb("top", [P, NT, 8])
        topi = sb("topi", [P, NT, 8], U32)

        start = probs[:].rearrange("p k a h q -> p (k a h q)")
        wmod_sb = start[:, 0:6 * C]
        wraw = start[:, 6 * C:8 * C].rearrange("p (w c) -> p w c", c=C)

        routing = qs[:].rearrange("p r q t -> p (r q t)")
        used_routing = [0]

        def routing_buf(dt, *dims):
            n = int(np.prod(dims)) * (2 if dt == F32 else 1)
            v = routing[:, used_routing[0]:used_routing[0] + n]
            used_routing[0] += n
            v = v.bitcast(dt) if dt == F32 else v
            names = " ".join("abc"[:len(dims)])
            return v.rearrange(f"p ({names}) -> p {names}", **{k: d for k, d in zip("abc", dims)})

        place = routing_buf(F32, NT, E)
        picked = routing_buf(F32, TOPK, NT, E)
        pos = routing_buf(F32, 5, TOPK * NT)
        inv = routing_buf(F32, 5, NTILE)
        inv_rhs = routing_buf(BF16, 2, TOPK * NT, NTILE)
        inv_sel = routing_buf(BF16, TOPK * NT, NTILE)

        moe = kd[:].rearrange("p r h q t -> p (r h q t)").bitcast(F32)
        used_moe = [0]

        def moe_buf(n):
            v = moe[:, used_moe[0]:used_moe[0] + n]
            used_moe[0] += n
            return v

        xs = moe_buf(TRING * C).rearrange("p (r c) -> p r c", c=C)
        xsT = moe_buf(TRING * P).rearrange("p (r c) -> p r c", c=P)
        ys = moe_buf(TRING * C).rearrange("p (r c) -> p r c", c=C)
        gate_act = moe_buf(TRING * I).rearrange("p (r i) -> p r i", i=I)
        hid = moe_buf(TRING * I).rearrange("p (r i) -> p r i", i=I)
        ybuf = probs[:].rearrange("p k a h q -> p (k a h q)")
        w1_t, w3_t, w2_t = (ybuf[:, i * TRING * I:(i + 1) * TRING * I].rearrange("c (r i) -> c r i", i=I) for i in range(3))
        assert NC * P == I and 3 * TRING * I + TOPK * NT * P // 2 <= ybuf.shape[1]
        inv_lhs = ybuf[:, 3 * TRING * I:3 * TRING * I + TOPK * NT * P // 2].bitcast(BF16).rearrange("p (k r) -> p k r", r=P)
        y01 = ybuf[:, 0:TOPK * NT * C].rearrange("p (k t c) -> p k t c", k=TOPK, c=C)
        comb = ybuf[:, TOPK * NT * C:(TOPK + 1) * NT * C].rearrange("p (t c) -> p t c", c=C)
        outb = ybuf[:, (TOPK + 1) * NT * C:(TOPK + 2) * NT * C].rearrange("p (t c) -> p t c", c=C)

        psA = ctx.enter_context(nc.psum_tensor("psA", [P, 2, 2, 512], F32))
        psB = ctx.enter_context(nc.psum_tensor("psB", [P, 2, 512], F32))
        psO = ctx.enter_context(nc.psum_tensor("psO", [P, 2, L], F32))
        psM = ctx.enter_context(nc.psum_tensor("psM", [P, 512], F32))

        psG, psU = (psA[:, 0, 0, :], psA[:, 1, 0, :], psB[:, 0, :]), (psA[:, 0, 1, :], psA[:, 1, 1, :], psB[:, 1, :])
        psX, psY = psO[:, 0, 0:P], psM[:, 0:C]
        psR = psB[:, 1, :]

        def late(b):
            return psA[:, 0, 0, :] if b == B - 1 else psM


        gathered = [sem(f"gathered{r}") for r in range(TRING)]
        scattered = [sem(f"scattered{r}") for r in range(TRING)]
        s = {n: sem(n) for n in (
            "moe_w route_const iota_steps picks_ready rank_ps pos_steps sel_ready rhs0_ready rhs1_ready lhs_ready inv_ps idx_ready te_ready wt_steps wt_exp "
            "gidx_first gidx_next sidx_ready xsT_first xsT_ps xsT_ready g_ps u_ps silu_ready hid_ready w3_ready y_ps y_ready "
            "y_in0 y_in1 y_in2 y_in3 y0_scaled comb_ready out_ready0 out_ready1 out_ready2 out_ready3 out_stored "
            "x_in0 x_in1 x_in2 c_in wmod_in0 wmod_in1 w_in wo_in consts masks cT_ps e_c silu_c silu_steps modT_ps modrow_ps modT_ok mod_steps mod_stored wqk_ok "
            "ln1_steps veps_ok rstd_ok stack_zero0 stack_zero1 one_rows0 one_rows1 vx_const "
            "xn_ready xnT_ps hT_ready qk_ps qkf_ready part_cast residuals parts_stored v_ps v_ready "
            "scoresA rowmax half_max mT_ps mT_ready emin_ready m_in0 m_in1 "
            "scoresB exped masked pv o_ready oT_ps den_steps normed aT_ps aT_ready op_ps t1_ready xg_ready x1_ready "
            "ln2_steps rs2_ready xn2_ready h2m_ready h2_ready h2T_ps h2T_ready lg_ps lg_ready top_ready h2_stored0 h2_stored1"
        ).split()}
        mod_in = [sem(f"mod_in{b}") for b in range(B)]
        stack_in = [sem(f"stack_in{i}") for i in range(RING)]
        block = ctx.enter_context(nc.Block())

        tok = lambda ap: ap.rearrange("b (t p) c -> p (b t) c", p=P)
        rounds = NTILE // TRING - 1
        NLOADS = 2 * 2 * 3

        @block.sync
        def _(sp):
            def load_x(i, lo, hi):
                sp.dma_start(x_sb[:, lo:hi, :], tok(x)[:, lo:hi, :]).then_inc(s[f"x_in{i}"], 16)

            load_x(0, 0, 2)
            sp.dma_start(wraw[:, 0, :], wq).then_inc(s["w_in"], 16)
            sp.dma_start(wraw[:, 1, :], wk).then_inc(s["w_in"], 16)
            sp.dma_start(wv_sb[:], wv).then_inc(s["w_in"], 16)
            sp.dma_start(bv_sb[:], bv.partition_broadcast(P)).then_inc(s["w_in"], 16)
            for i, bias in enumerate((bq, bk)):
                for h in range(H2):
                    sp.dma_start(bqk[64 * h:64 * h + 64, i:i + 1],
                                 bias.rearrange("(p h d o) -> h d p o", p=NPAIR, h=H2, o=1)[h],
                                 allow_slow_non_contiguous=True).then_inc(s["w_in"], 16)
            load_x(1, 2, 6)
            load_x(2, 6, NT)
            sp.dma_start(wo_sb[:], wo).then_inc(s["wo_in"], 16)
            sp.dma_start(gate_sb[:], gate).then_inc(s["wo_in"], 16)

            def store_max(b, half):
                sp.wait_ge(s["mT_ready"], 2 * b + half + 1)
                sp.dma_start(qs[SROWS:SROWS + H2, b % RING, 4 * half:4 * half + 4, :],
                             mT[:, b % 2, half, :]).then_inc(s[f"m_in{half}"], 16)

            def store_parts(b):
                sp.wait_ge(s["residuals"], 3 * b + 3)
                sp.dma_start(parts_d[b].rearrange("w s c t -> c (w s) t"),
                             parts[:].rearrange("c w s t -> c (w s) t")).then_inc(s["parts_stored"], 16)

            def fill_stacks(b):
                sp.wait_ge(s["parts_stored"], 16 * b + 16)
                if b < 2:
                    sp.wait_ge(s[f"stack_zero{b}"], 2 + b)
                    sp.wait_ge(s[f"one_rows{b}"], 2)
                if b >= RING:
                    sp.wait_ge(s["scoresB"], 16 * (b - RING + 1))
                r = b % RING
                for h in range(H2):
                    q_src, k_src = (parts_d[b, side].rearrange("s (h d p) t -> h s d (p t)", h=H2, d=D)[h] for side in range(2))
                    q_dst = qs[h * HROWS:(h + 1) * HROWS, r].rearrange("r p t -> r (p t)")
                    k_dst = kd[h * HROWS:(h + 1) * HROWS, r, h].rearrange("r p t -> r (p t)")
                    for slot, n in ((0, 3), (3, 2), (5, 1)):
                        part = QP[slot]
                        sp.dma_start(q_dst[slot * D:(slot + n) * D],
                                     q_src[part:part + 1].broadcast_to([n, D, NPAIR * L])).then_inc(stack_in[r], 16)
                        sp.dma_start(k_dst[slot * D:(slot + n) * D], k_src[0:n]).then_inc(stack_in[r], 16)

            def load_experts(e):
                for w_sb, w in ((w1_sb, w1), (w3_sb, w3)):
                    sp.dma_start(w_sb[:, e:e + 2], w[e:e + 2].rearrange("e c i -> c e i")).then_inc(s["moe_w"], 16)
                sp.dma_start(w2_sb[:, e:e + 2].rearrange("p e k c -> p (e k) c"),
                             w2[e:e + 2].rearrange("e (k p) c -> p (e k) c", p=P)).then_inc(s["moe_w"], 16)

            def store_mod_rows():
                sp.wait_ge(s["mod_steps"], 7)
                sp.dma_start(mod_d, modrow[:, 0:5, :].rearrange("b r c -> b (r c)")).then_inc(s["mod_stored"], 16)

            def broadcast_mod_rows(b):
                sp.wait_ge(s["mod_stored"], 16)
                sp.dma_start(mod_sb[:, b].rearrange("p r c -> p (r c)"), mod_d[b].partition_broadcast(P)).then_inc(mod_in[b], 16)

            for step in range(-AHEAD, B + 4):
                if step == 0:
                    store_mod_rows()
                if 2 <= step < 2 + E // 2:
                    load_experts(2 * (step - 2))
                if 0 <= step - 1 < B:
                    store_max(step - 1, 1)
                if 0 <= step + AHEAD - 1 < B:
                    fill_stacks(step + AHEAD - 1)
                if 0 <= step + AHEAD < B:
                    store_parts(step + AHEAD)
                if 0 <= step < B:
                    store_max(step, 0)
                    broadcast_mod_rows(step)
                if 0 <= step - 3 < B:
                    a = step - 3
                    sp.wait_ge(s["h2_ready"], a + 1)
                    sp.dma_start(h2_d.rearrange("(b t p) c -> b p t c", t=2, p=P)[a], h2[:, a % 2]).then_inc(s[f"h2_stored{a % 2}"], 16)
            for i in range(2):
                sp.wait_ge(s[f"h2_stored{i}"], 16 * (B // 2))
            for r in range(TRING):
                sp.wait_ge(scattered[r], 16 * (NTILE // TRING))
            n = NT // 4
            y_t = y_d[0:TOPK * NTOK].rearrange("(k t p) c -> p k t c", k=TOPK, p=P)
            for i in range(4):
                for k in range(TOPK):
                    sp.dma_start(y01[:, k, n * i:n * i + n], y_t[:, k, n * i:n * i + n]).then_inc(s[f"y_in{i}"], 16)
            for i in range(4):
                sp.wait_ge(s[f"out_ready{i}"], 1)
                sp.dma_start(tok(out)[:, n * i:n * i + n], outb[:, n * i:n * i + n]).then_inc(s["out_stored"], 16)
            sp.wait_ge(s["out_stored"], 64)

        @block.scalar
        def _(act):
            act.dma_start(c_sb[:], c).then_inc(s["c_in"], 16)
            act.dma_start(wmod_sb[:, 0:2 * C], wmod[:, 0:2 * C]).then_inc(s["wmod_in0"], 16)
            act.wait_ge(s["cT_ps"], 1)
            nc.scalar.activation(cT[:, 1, :], psM[:, 0:B], ACT.Exp, scale=-1.0).then_inc(s["e_c"], 1)
            act.dma_start(wmod_sb[:, 2 * C:6 * C], wmod[:, 2 * C:6 * C]).then_inc(s["wmod_in1"], 16)
            act.dma_start(bo8[:], bo.partition_broadcast(B)).then_inc(s["wmod_in1"], 16)

            def modulate(b):
                act.wait_ge(s["xnT_ps"], b + 1)
                if b == 0:
                    act.wait_ge(s["modT_ok"], 2)
                if b >= 1:
                    act.wait_ge(s["v_ps"], b)
                nc.scalar.activation(hT[:], psM[:, 0:L], ACT.Identity, scale=modT[:, 1, b:b + 1],
                                     bias=modT[:, 0, b:b + 1]).then_inc(s["hT_ready"], 1)

            def qk_copy(b):
                act.wait_ge(s["qk_ps"], b + 1)
                if b == 0:
                    act.wait_ge(s["wqk_ok"], 3)
                if b >= 1:
                    act.wait_ge(s["residuals"], 3 * b)
                nc.scalar.activation(qkf[:, 0, :], psM[:, 0:L], ACT.Identity, bias=bqk[:, 2:3],
                                     scale=float(D) ** -0.5).then_inc(s["qkf_ready"], 1)
                nc.scalar.activation(qkf[:, 1, :], psM[:, L:2 * L], ACT.Identity,
                                     bias=bqk[:, 1:2]).then_inc(s["qkf_ready"], 1)

            def cast_part(b):
                act.wait_ge(s["qkf_ready"], 2 * b + 2)
                if b >= 1:
                    act.wait_ge(s["parts_stored"], 16 * b)
                nc.scalar.copy(parts[:, :, 0, :], qkf[:]).then_inc(s["part_cast"], 1)

            def m_copy(b, half):
                act.wait_ge(s["mT_ps"], 2 * b + half + 1)
                if b >= 2:
                    act.wait_ge(s[f"m_in{half}"], 16 * (b - 1))
                nc.scalar.copy(mT[:, b % 2, half, :], psM[0:8, 0:P].bitcast(BF16)).then_inc(s["mT_ready"], 1)
                if b >= 3:
                    act.wait_ge(s["den_steps"], 3 * (b - 2))
                nc.scalar.activation(emin[:, b % 3, half], negmb[:, b % 2, half], ACT.Exp).then_inc(s["emin_ready"], 1)

            def exps(b, j):
                n = NPAIR * b + j
                if n == 0:
                    act.wait_ge(s["wqk_ok"], 2)
                    act.wait_ge(s["modrow_ps"], 1)
                for kt in range(2):
                    act.wait_ge(s["scoresB"], 2 * n + kt + 1)
                    if n >= PRING and j % 4 == 0:
                        act.wait_ge(s["pv"], 4 * (n // 4 - 1))
                    nc.scalar.activation(probs[:, kt, n % PRING], psB[:, kt, :].rearrange("p (h q) -> p h q", h=H2),
                                         ACT.Exp).then_inc(s["exped"], 1)

            def o_copy(b):
                act.wait_ge(s["pv"], 8 * (b + 1))
                if b >= 1:
                    act.wait_ge(s["oT_ps"], b)
                nc.scalar.copy(oS[:], psO[:]).then_inc(s["o_ready"], 1)

            def aT_copy(b):
                act.wait_ge(s["aT_ps"], b + 1)
                if b >= 1:
                    act.wait_ge(s["op_ps"], b)
                nc.scalar.copy(aT[:], late(b)[:, 0:L]).then_inc(s["aT_ready"], 1)

            def h2T_copy(b):
                act.wait_ge(s["h2T_ps"], b + 1)
                if b >= 1:
                    act.wait_ge(s["lg_ps"], b)
                nc.scalar.copy(h2T[:], late(b)[:, 0:L]).then_inc(s["h2T_ready"], 1)

            for step in range(-AHEAD, B + 4):
                has = lambda b: 0 <= b < B
                for j in range(NPAIR):
                    if j == 0 and has(step - 4):
                        h2T_copy(step - 4)
                    if j == 0 and has(step + AHEAD):
                        modulate(step + AHEAD)
                    if j == 2 and has(step - 1):
                        m_copy(step - 1, 1)
                    if j == 3 and has(step + AHEAD):
                        qk_copy(step + AHEAD)
                    if j == 4 and has(step + AHEAD):
                        cast_part(step + AHEAD)
                    if j == 5 and has(step):
                        m_copy(step, 0)
                    if j == 7 and has(step - 2):
                        aT_copy(step - 2)
                    if has(step - 1):
                        exps(step - 1, j)
                    if j == 3 and has(step - 2):
                        o_copy(step - 2)

            act.wait_ge(s["sel_ready"], 1)
            nc.scalar.activation(inv_rhs[:, 0], inv_sel[:], ACT.Copy, scale=iota_p[:, 0:1]).then_inc(s["rhs0_ready"], 1)
            act.wait_ge(s["wt_steps"], 1)
            nc.scalar.activation(wts[:, 1, :], wts[:, 0, :], ACT.Exp).then_inc(s["wt_exp"], 1)

            def silu(m, r):
                act.wait_ge(s["g_ps"], m + 1)
                nc.scalar.activation(gate_act[:, r], psG[r], ACT.Silu).then_inc(s["silu_ready"], 1)

            def y_copy(n, r, turn):
                act.wait_ge(s["y_ps"], n + 1)
                if not first(turn):
                    act.wait_ge(scattered[r], 16 * turn)
                nc.scalar.copy(ys[:, r], psY).then_inc(s["y_ready"], 1)

            def w3_copy(n, r):
                e = act.value_load(tile_e[0:1, bass.ds(n, 1)], min_val=0, max_val=E - 1)
                nc.scalar.copy(w3_t[:, r], w3_sb[:, bass.ds(e, 1), :].rearrange("c o i -> c (o i)")).then_inc(s["w3_ready"], 1)

            act.wait_ge(s["te_ready"], 1)
            act.wait_ge(s["moe_w"], 16 * 3 * (E // 2))
            act.wait_ge(s["lhs_ready"], 2 * NT)
            w3_copy(0, 0)
            w3_copy(1, 1)
            silu(0, 0)

            def three_tiles(it):
                for r in range(TRING):
                    n = it * TRING + r
                    if not first(n):
                        act.wait_ge(s["u_ps"], n)
                    w3_copy(n + 2, (r + 2) % TRING)
                    silu(n + 1, (r + 1) % TRING)
                    y_copy(n, r, it)

            three_tiles(0)
            with act.Fori(1, rounds) as it:
                three_tiles(it)
            act.wait_ge(s["u_ps"], rounds * TRING)
            w3_copy(NTILE - 1, 2)
            for r in range(TRING):
                if r < TRING - 1:
                    silu(rounds * TRING + r + 1, r + 1)
                y_copy(rounds * TRING + r, r, rounds)

            for i in range(4):
                act.wait_ge(s[f"y_in{i}"], 32)
                n = NT // 4
                for j in range(n * i, n * i + n):
                    act.activation(y01[:, 0, j], y01[:, 0, j], ACT.Copy, scale=wts[:, 2, j:j + 1]).then_inc(s["y0_scaled"], 1)

        @block.gpsimd
        def _(pool):
            nc.gpsimd.memset(ident[:], 0.0).then_inc(s["masks"], 1)
            nc.gpsimd.memset(ident_b[:], 0.0).then_inc(s["masks"], 1)
            nc.gpsimd.memset(mask_b[:], 0.0).then_inc(s["masks"], 1)
            nc.gpsimd.memset(npad[:], 0.0).then_inc(s["masks"], 1)
            nc.gpsimd.memset(neghalf[:], -0.5).then_inc(s["masks"], 1)
            pool.wait_ge(s["masks"], 5)
            for t in (ident, ident_b):
                nc.gpsimd.affine_select(out=t[:], in_=t[:], compare_op=ALU.not_equal, fill=1.0, base=0,
                                        pattern=[[-1, P]], channel_multiplier=1).then_inc(s["consts"], 1)
            for qt, sign in ((0, 1), (1, -1)):
                nc.gpsimd.affine_select(out=mask_b[:, qt], in_=mask_b[:, qt], compare_op=ALU.is_ge, fill=MASKED, base=0,
                                        pattern=[[0, H2], [-sign, P]], channel_multiplier=sign).then_inc(s["consts"], 1)
            nc.gpsimd.iota(npad_i[:, 0:1], [[0, 1]], base=P, channel_multiplier=-1).then_inc(s["masks"], 1)
            nc.gpsimd.iota(npad_i[:, 1:2], [[0, 1]], base=1, channel_multiplier=1).then_inc(s["masks"], 1)
            pool.wait_ge(s["masks"], 7)
            nc.gpsimd.tensor_copy(npad[:], npad_i[:]).then_inc(s["consts"], 1)
            nc.gpsimd.memset(vx[:], 0.0).then_inc(s["vx_const"], 1)
            pool.wait_ge(s["vx_const"], 1)
            for par in range(H2):
                nc.gpsimd.memset(vx[:, :, :, :, par, 16 + par:17 + par].rearrange("p r k q o -> p (r k q) o"),
                                 1.0).then_inc(s["vx_const"], 1)

            def ln1_rstd(b):
                pool.wait_ge(s["veps_ok"], b + 1)
                nc.gpsimd.tensor_tensor(rstd[:, 2 * b:2 * b + 2], veps[:, 2 * b:2 * b + 2], neghalf[:, 0:2],
                                        ALU.pow).then_inc(s["rstd_ok"], 1)

            ln1_rstd(0)
            nc.gpsimd.memset(kd[:, 1].rearrange("p h q t -> p (h q t)"), 0.0).then_inc(s["stack_zero1"], 1)
            pool.wait_ge(s["stack_zero1"], 1)
            ln1_rstd(1)
            nc.gpsimd.memset(kd[:, 2].rearrange("p h q t -> p (h q t)"), 0.0).then_inc(s["stack_zero1"], 1)
            pool.wait_ge(s["stack_zero1"], 2)
            nc.gpsimd.memset(qs[96:128, 1:].rearrange("p r q t -> p (r q t)"), 0.0).then_inc(s["stack_zero1"], 1)
            pool.wait_ge(s["stack_zero1"], 3)

            def mask_probs(b, j):
                n = NPAIR * b + j
                v = probs[:, :, n % PRING:n % PRING + 2].rearrange("p k a h q -> p k (a h) q")
                pool.wait_ge(s["exped"], 2 * n + 4)
                for kt, sign in ((0, 1), (1, -1)):
                    u = v[:, kt, :, P:2 * P] if kt == 0 else v[:, kt, :, 0:P]
                    nc.gpsimd.affine_select(out=u, in_=u, compare_op=ALU.is_ge, fill=0.0, base=0,
                                            pattern=[[0, 2 * H2], [-sign, P]], channel_multiplier=sign).then_inc(s["masked"], 1)

            def xg(b):
                for t in range(2):
                    v = x_sb[:, 2 * b + t, :]
                    last = nc.gpsimd.tensor_tensor(v, v, mod_sb[:, b, 4, :], ALU.add)
                last.then_inc(s["xg_ready"], 1)

            def x1_sum(b):
                pool.wait_ge(s["t1_ready"], 2 * b + 2)
                pool.wait_ge(s["xg_ready"], b + 1)
                nc.gpsimd.tensor_tensor(x_sb[:, 2 * b:2 * b + 2, :], t1[:], x_sb[:, 2 * b:2 * b + 2, :],
                                        ALU.add).then_inc(s["x1_ready"], 1)

            def ln2_rstd(b):
                pool.wait_ge(s["ln2_steps"], 3 * b + 3)
                nc.gpsimd.tensor_tensor(rs2[:], ve2[:], neghalf[:, 0:2], ALU.pow).then_inc(s["rs2_ready"], 1)

            def h2_scale(b):
                pool.wait_ge(s["xn2_ready"], 2 * b + 2)
                if b >= 1:
                    pool.wait_ge(s["h2_ready"], b)
                for t in range(2):
                    nc.gpsimd.tensor_tensor(h2m[:, t], xn2[:, t], mod_sb[:, b, 2, :], ALU.mult).then_inc(s["h2m_ready"], 1)

            def h2_shift(b):
                if b >= 2:
                    pool.wait_ge(s[f"h2_stored{b % 2}"], 16 * (b // 2))
                    pool.wait_ge(s["h2T_ps"], b - 1)
                pool.wait_ge(s["h2m_ready"], 2 * b + 2)
                for t in range(2):
                    last = nc.gpsimd.tensor_tensor(h2[:, b % 2, t], h2m[:, t], mod_sb[:, b, 1, :], ALU.add)
                last.then_inc(s["h2_ready"], 1)

            v = iotas[:]
            for lo, n, pattern, base, mult in ((0, P, [[1, P]], 0, 0), (P, 1, [[0, 1]], 0, 1), (P + 1, TOPK * NT, [[1, TOPK * NT]], 1, 0),
                                               (P + 64, NTILE, [[P, NTILE]], (TOPK * NTOK) + P, 1)):
                nc.gpsimd.iota(v[:, lo:lo + n], pattern, base=base, channel_multiplier=mult).then_inc(s["iota_steps"], 1)
            pool.wait_ge(s["iota_steps"], 4)
            for dst, lo, n in ((iota_e, 0, E), (iota_a, 0, NTILE), (iota_c, 0, P), (iota_p, P, 1), (iota_kt, P + 1, TOPK * NT),
                               (dump_row, P + 64, NTILE)):
                nc.gpsimd.tensor_copy(dst[:], v[:, lo:lo + n]).then_inc(s["route_const"], 1)
            nc.gpsimd.memset(ones_b[:], 1.0).then_inc(s["route_const"], 1)
            nc.gpsimd.memset(before[:, 0, :], 0.0).then_inc(s["route_const"], 1)
            nc.gpsimd.memset(upto[:], 0.0).then_inc(s["route_const"], 1)
            pool.wait_ge(s["route_const"], 9)
            nc.gpsimd.affine_select(out=tri[:], in_=ones_b[:], compare_op=ALU.is_gt, fill=0.0, base=0,
                                    pattern=[[1, P]], channel_multiplier=-1).then_inc(s["route_const"], 1)

            for step in range(-AHEAD, B + 4):
                has = lambda b: 0 <= b < B
                for j in range(NPAIR):
                    if j == 3 and has(step - 3):
                        ln2_rstd(step - 3)
                    if j == 1 and has(step - 3) and step - 3 < B - 1:
                        x1_sum(step - 3)
                    if j % 2 == 1 and has(step - 1):
                        mask_probs(step - 1, j - 1)
                    if j == 2 and step > -AHEAD and has(step + AHEAD + 1):
                        ln1_rstd(step + AHEAD + 1)
                    if j == 4 and has(step - 3) and step - 3 < B - 1:
                        h2_scale(step - 3)
                    if j == 5 and has(step - 3) and step - 3 < B - 1:
                        h2_shift(step - 3)
                    if j == 6 and has(step - 1):
                        b = step - 1
                        pool.wait_ge(mod_in[b], 16)
                        pool.wait_ge(s["xn_ready"], b + 1)
                        xg(b)

            nkt = TOPK * NT
            pool.wait_ge(s["sel_ready"], 1)
            nc.gpsimd.tensor_tensor(inv_rhs[:, 1], inv_sel[:], iota_kt[:].rearrange("p (k o) -> p k o", o=1).broadcast_to([P, nkt, NTILE]),
                                    ALU.mult).then_inc(s["rhs1_ready"], 1)

            pool.wait_ge(s["idx_ready"], 2)
            for i in range(2):
                pool.wait_ge(s[f"h2_stored{i}"], 16 * (B // 2))

            def table_ready():
                pool.wait_ge(s["idx_ready"], 2)

            def gather(n, r, copied, count):
                table_ready()
                nc.gpsimd.tensor_copy(gidx[r][:], gat_idx[:, bass.ds(n, 1)]).then_inc(s[copied], 1)
                table_ready()
                pool.wait_ge(s[copied], count)
                pool.indirect_dma_start(xs[:, r], None, h2_d, bass.IndirectOffsetOnAxis(ap=gidx[r][:, 0:1], axis=0)).then_inc(gathered[r], 16)

            def scatter(n, r, turn):
                if not first(turn):
                    pool.wait_ge(scattered[r], 16 * turn)
                table_ready()
                nc.gpsimd.tensor_copy(sidx[r][:], sca_idx[:, bass.ds(n, 1)]).then_inc(s["sidx_ready"], 1)
                table_ready()
                pool.wait_ge(s["sidx_ready"], n + 1)
                pool.wait_ge(s["y_ready"], n + 1)
                pool.indirect_dma_start(y_d, bass.IndirectOffsetOnAxis(ap=sidx[r][:, 0:1], axis=0), ys[:, r], None).then_inc(scattered[r], 16)

            for r in range(TRING):
                gather(r, r, "gidx_first", r + 1)
            pool.wait_ge(s["xsT_first"], 1)
            gather(TRING, 0, "gidx_first", TRING + 1)

            def gather_ahead(n, r):
                pool.wait_ge(s["xsT_ps"], n + 1)
                gather(n + 4, (r + 4) % TRING, "gidx_next", n + 1)

            def three_tiles(it):
                for r in range(TRING):
                    n = it * TRING + r
                    gather_ahead(n, r)
                    scatter(n, r, it)

            three_tiles(0)
            with pool.Fori(1, rounds - 1) as it:
                three_tiles(it)
            for n in range((rounds - 1) * TRING, NTILE):
                if n + 4 < NTILE:
                    gather_ahead(n, n % TRING)
                scatter(n, n % TRING, n // TRING)
            for i in range(3):
                tt = slice(NT // 4 * i, NT // 4 * (i + 1))
                pool.wait_ge(s["comb_ready"], i + 1)
                nc.gpsimd.tensor_tensor(outb[:, tt], comb[:, tt], x_sb[:, tt], ALU.add).then_inc(s[f"out_ready{i}"], 1)

        @block.vector
        def _(dve):
            def ln1_stats(b):
                if b in (0, 1, 3):
                    dve.wait_ge(s[f"x_in{min(b, 2)}"], 16)
                for i in range(2 * b, 2 * b + 2):
                    last = nc.vector.bn_stats(stats[:, i, :], x_sb[:, i, :])
                last.then_inc(s["ln1_steps"], 1)
                dve.wait_ge(s["ln1_steps"], 2 * b + 1)
                for i in range(2 * b, 2 * b + 2):
                    last = nc.vector.bn_aggr(mv[:, i, :], stats[:, i, :])
                last.then_inc(s["ln1_steps"], 1)
                dve.wait_ge(s["ln1_steps"], 2 * b + 2)
                nc.vector.tensor_scalar(veps[:, 2 * b:2 * b + 2], mv[:, 2 * b:2 * b + 2, 1], EPS, None,
                                        ALU.add).then_inc(s["veps_ok"], 1)

            def normalise(b):
                dve.wait_ge(s["rstd_ok"], b + 1)
                if b >= 2:
                    dve.wait_ge(s["xnT_ps"], b - 1)
                for t in range(2):
                    i = 2 * b + t
                    last = nc.vector.tensor_scalar(xn[:, b % 2, t, :], x_sb[:, i, :], mv[:, i, 0:1], rstd[:, i:i + 1],
                                                   ALU.subtract, ALU.mult)
                last.then_inc(s["xn_ready"], 1)

            nc.vector.memset(kd[:, 0].rearrange("p h q t -> p (h q t)"), 0.0).then_inc(s["stack_zero0"], 1)
            nc.vector.memset(qs[96:128, 0].rearrange("p q t -> p (q t)"), 0.0).then_inc(s["stack_zero0"], 1)
            dve.wait_ge(s["stack_zero0"], 1)
            dve.wait_ge(s["consts"], 1)

            def one_rows(slots, done):
                for h in range(H2):
                    v = kd[96:128, slots, h].rearrange("p r q t -> p r (q t)")
                    nc.vector.tensor_scalar(v, v, ident[96:128, 96 + h:97 + h], None, ALU.add).then_inc(s[done], 1)

            one_rows(slice(0, 1), "one_rows0")
            ln1_stats(0)
            dve.wait_ge(s["e_c"], 1)
            nc.vector.tensor_scalar(cT[:, 0, :], cT[:, 1, :], 1.0, None, ALU.add).then_inc(s["silu_steps"], 1)
            dve.wait_ge(s["silu_steps"], 1)
            nc.vector.reciprocal(cT[:, 2, :], cT[:, 0, :]).then_inc(s["silu_steps"], 1)
            dve.wait_ge(s["silu_steps"], 2)
            nc.vector.tensor_tensor(cT[:, 3, :], psM[:, 0:B], cT[:, 2, :], ALU.mult).then_inc(s["silu_c"], 1)
            normalise(0)
            dve.wait_ge(s["modT_ps"], 1)
            nc.vector.tensor_copy(modT[:, 0, :], psM[:, 0:B]).then_inc(s["modT_ok"], 1)
            nc.vector.tensor_scalar(modT[:, 1, :], psM[:, B:2 * B], 1.0, None, ALU.add).then_inc(s["modT_ok"], 1)
            dve.wait_ge(s["w_in"], 16 * 8)
            for i in range(2):
                nc.vector.tensor_copy(wqk[:, i, :].rearrange("c (h d p) -> c h d p", h=H2, d=D),
                                      wraw[:, i, :].rearrange("c (p h d) -> c h d p", h=H2, d=D)).then_inc(s["wqk_ok"], 1)
            nc.vector.tensor_scalar(bqk[:, 2:3], bqk[:, 0:1], float(D) ** -0.5, None, ALU.mult).then_inc(s["wqk_ok"], 1)

            def mod_rows():
                ps = psO[0:B].rearrange("b h q -> b (h q)").rearrange("b (r c) -> b r c", c=C)
                dve.wait_ge(s["modrow_ps"], 1)
                nc.vector.tensor_copy(modrow[:, 1, :], ps[:, 1, :]).then_inc(s["mod_steps"], 1)
                nc.vector.tensor_scalar(modrow[:, 2, :], ps[:, 2, :], 1.0, None, ALU.add).then_inc(s["mod_steps"], 1)
                sign, gates, g = modrow[:, 5:7, :], modrow[:, 0:4:3, :], ps[:, 0:4:3, :]
                nc.vector.tensor_scalar(sign, g, 0.0, 2.0, ALU.is_ge, ALU.mult).then_inc(s["mod_steps"], 1)
                dve.wait_ge(s["mod_steps"], 3)
                nc.vector.tensor_scalar(sign, sign, -1.0, None, ALU.add).then_inc(s["mod_steps"], 1)
                dve.wait_ge(s["mod_steps"], 4)
                nc.vector.tensor_tensor(gates, g, sign, ALU.mult).then_inc(s["mod_steps"], 1)
                dve.wait_ge(s["mod_steps"], 5)
                nc.vector.scalar_tensor_tensor(out=gates, in0=gates, scalar=0.25, in1=sign,
                                               op0=ALU.max, op1=ALU.mult).then_inc(s["mod_steps"], 1)
                dve.wait_ge(s["mod_steps"], 6)
                nc.vector.tensor_tensor(modrow[:, 4, :], modrow[:, 0, :], bo8[:], ALU.mult).then_inc(s["mod_steps"], 1)

            def split(b, i):
                if i == 0:
                    dve.wait_ge(s["part_cast"], b + 1)
                    nc.vector.tensor_tensor(resid[:], qkf[:], parts[:, :, 0, :], ALU.subtract).then_inc(s["residuals"], 1)
                    dve.wait_ge(s["residuals"], 3 * b + 1)
                    if b >= 1:
                        dve.wait_ge(s["parts_stored"], 16 * b)
                    nc.vector.tensor_copy(parts[:, :, 1, :], resid[:]).then_inc(s["residuals"], 1)
                else:
                    dve.wait_ge(s["residuals"], 3 * b + 2)
                    nc.vector.tensor_tensor(parts[:, :, 2, :], resid[:], parts[:, :, 1, :], ALU.subtract).then_inc(s["residuals"], 1)

            def values(b):
                dve.wait_ge(s["v_ps"], b + 1)
                if b == 0:
                    dve.wait_ge(s["vx_const"], 3)
                if b >= VRING:
                    dve.wait_ge(s["pv"], 8 * (b - VRING + 1))
                for kt in range(2):
                    for par in range(H2):
                        last = nc.vector.tensor_tensor(
                            vx[:, b % VRING, kt, :, par, D * par:D * par + D],
                            psM[:, kt * C:(kt + 1) * C].rearrange("p (q h d) -> p q h d", h=H2, d=D)[:, :, par, :],
                            bv_sb[:].rearrange("p (q h d) -> p q h d", h=H2, d=D)[:, :, par, :], ALU.add)
                last.then_inc(s["v_ready"], 1)

            def row_max(b, j):
                n = NPAIR * b + j
                dve.wait_ge(s["scoresA"], n + 1)
                if j == 0 and b >= 2:
                    dve.wait_ge(s["half_max"], 2 * (b - 1))
                nc.vector.tensor_reduce(negm[:, b % 2, :, :, j],
                                        psA[:, n % 2].rearrange("p q (h k) -> p q h k", h=H2),
                                        AX.X, ALU.max, negate=True).then_inc(s["rowmax"], 1)

            def half_max(b, half):
                dve.wait_ge(s["rowmax"], NPAIR * b + 4 * half + 4)
                if b >= 2:
                    dve.wait_ge(s["mT_ps"], 2 * (b - 2) + half + 1)
                    dve.wait_ge(s["emin_ready"], 2 * (b - 2) + half + 1)
                for qt in range(2):
                    last = nc.vector.tensor_scalar(negmb[:, b % 2, half, qt], negm[:, b % 2, qt, :, 4 * half:4 * half + 4],
                                                   0.0, None, ALU.min)
                last.then_inc(s["half_max"], 1)

            def pad_term(b):
                dve.wait_ge(s["emin_ready"], 2 * b + 2)
                if b == 0:
                    dve.wait_ge(s["consts"], 5)
                for qt in range(2):
                    last = nc.vector.tensor_scalar(
                        den[:, 0, qt, :].rearrange("p (f q h) -> p f h q", f=2, h=H2),
                        emin[:, b % 3, :, qt], npad[:, qt:qt + 1], None, ALU.mult)
                last.then_inc(s["den_steps"], 1)

            def normalise_attn(b):
                dve.wait_ge(s["den_steps"], 3 * b + 1)
                dve.wait_ge(s["oT_ps"], b + 1)
                for qt in range(2):
                    ps = late(b)[:, qt * 256:(qt + 1) * 256].rearrange("p (q r) -> p q r", r=VCOL)
                    last = nc.vector.tensor_tensor(
                        den[:, 1, qt, :].rearrange("p (q h) -> p q h", h=H2), ps[:, :, 16:18],
                        den[:, 0, qt, :].rearrange("p (q h) -> p q h", h=H2), ALU.add)
                last.then_inc(s["den_steps"], 1)
                dve.wait_ge(s["den_steps"], 3 * b + 2)
                nc.vector.reciprocal(den[:, 2], den[:, 1]).then_inc(s["den_steps"], 1)
                dve.wait_ge(s["den_steps"], 3 * b + 3)
                if b >= 1:
                    dve.wait_ge(s["aT_ps"], b)
                for qt in range(2):
                    ps = late(b)[:, qt * 256:(qt + 1) * 256].rearrange("p (q r) -> p q r", r=VCOL)[:, :, 0:16]
                    last = nc.vector.tensor_tensor(
                        attn[:, qt, :].rearrange("p (q h d) -> p q h d", h=H2, d=D),
                        ps.rearrange("p q (h d) -> p q h d", d=D),
                        den[:, 2, qt, :].rearrange("p (q h o) -> p q h o", h=H2, o=1).broadcast_to([P, NPAIR, H2, D]),
                        ALU.mult)
                last.then_inc(s["normed"], 1)

            def gate_attn(b):
                dve.wait_ge(mod_in[b], 16)
                dve.wait_ge(s["op_ps"], b + 1)
                if b >= 1:
                    dve.wait_ge(s["x1_ready"], b)
                for t in range(2):
                    nc.vector.tensor_tensor(t1[:, t], late(b)[:, t * C:(t + 1) * C], mod_sb[:, b, 0, :],
                                            ALU.mult).then_inc(s["t1_ready"], 1)

            def x1_last(b):
                dve.wait_ge(s["t1_ready"], 2 * b + 2)
                dve.wait_ge(s["xg_ready"], b + 1)
                v = x_sb[:, 2 * b:2 * b + 2, :]
                nc.vector.tensor_tensor(v, t1[:], v, ALU.add).then_inc(s["x1_ready"], 1)

            def h2_last(b):
                dve.wait_ge(s["xn2_ready"], 2 * b + 2)
                dve.wait_ge(s["h2_ready"], b)
                nc.vector.tensor_tensor(h2m[:], xn2[:], mod_sb[:, b, 2:3, :].broadcast_to([P, 2, C]), ALU.mult).then_inc(s["h2m_ready"], 2)
                dve.wait_ge(s["h2m_ready"], 2 * b + 2)
                dve.wait_ge(s[f"h2_stored{b % 2}"], 16 * (b // 2))
                dve.wait_ge(s["h2T_ps"], b - 1)
                nc.vector.tensor_tensor(h2[:, b % 2], h2m[:], mod_sb[:, b, 1:2, :].broadcast_to([P, 2, C]), ALU.add).then_inc(s["h2_ready"], 1)

            def ln2_stats(b):
                dve.wait_ge(s["x1_ready"], b + 1)
                for t in range(2):
                    last = nc.vector.bn_stats(stats2[:, t, :], x_sb[:, 2 * b + t, :])
                last.then_inc(s["ln2_steps"], 1)
                dve.wait_ge(s["ln2_steps"], 3 * b + 1)
                for t in range(2):
                    last = nc.vector.bn_aggr(mv2[:, t, :], stats2[:, t, :])
                last.then_inc(s["ln2_steps"], 1)
                dve.wait_ge(s["ln2_steps"], 3 * b + 2)
                if b >= 1:
                    dve.wait_ge(s["rs2_ready"], b)
                nc.vector.tensor_scalar(ve2[:], mv2[:, :, 1], EPS, None, ALU.add).then_inc(s["ln2_steps"], 1)

            def ln2_normalise(b):
                dve.wait_ge(s["rs2_ready"], b + 1)
                if b >= 1:
                    dve.wait_ge(s["h2m_ready"], 2 * b)
                for t in range(2):
                    nc.vector.tensor_scalar(xn2[:, t], x_sb[:, 2 * b + t, :], mv2[:, t, 0:1], rs2[:, t:t + 1],
                                            ALU.subtract, ALU.mult).then_inc(s["xn2_ready"], 1)

            def top2(b):
                dve.wait_ge(s["lg_ps"], b + 1)
                nc.vector.tensor_copy(lg[:, 2 * b:2 * b + 2, :],
                                      late(b)[:, 0:16].rearrange("p (t e) -> p t e", e=8)).then_inc(s["lg_ready"], 1)
                dve.wait_ge(s["lg_ready"], b + 1)
                for t in range(2 * b, 2 * b + 2):
                    last = nc.vector.max(top[:, t, :], lg[:, t, :])
                    last.then_inc(s["top_ready"], 1)
                dve.wait_ge(s["top_ready"], 4 * b + 2)
                for t in range(2 * b, 2 * b + 2):
                    nc.vector.max_index(topi[:, t, :], top[:, t, :], lg[:, t, :]).then_inc(s["top_ready"], 1)
                dve.wait_ge(s["top_ready"], 4 * b + 4)
                tt = slice(2 * b, 2 * b + 2)
                nc.vector.tensor_copy(topf[:, tt], topi[:, tt, 0:TOPK]).then_inc(s["picks_ready"], 1)
                dve.wait_ge(s["picks_ready"], 6 * b + 1)
                if b == 0:
                    dve.wait_ge(s["route_const"], 10)
                for k in range(TOPK):
                    nc.vector.tensor_tensor(pick[:, k, tt], iota_e[:].rearrange("p (o e) -> p o e", o=1).broadcast_to([P, 2, E]),
                                            topf[:, tt, k:k + 1].broadcast_to([P, 2, E]), ALU.is_equal).then_inc(s["picks_ready"], 1)
                dve.wait_ge(s["picks_ready"], 6 * b + 3)
                nc.vector.tensor_tensor(used[:, tt], pick[:, 0, tt], pick[:, 1, tt], ALU.add).then_inc(s["picks_ready"], 1)
                dve.wait_ge(s["picks_ready"], 6 * b + 4)
                for i in range(2):
                    nc.vector.tensor_tensor(before[:, 2 * b + i + 1], before[:, 2 * b + i], used[:, 2 * b + i],
                                            ALU.add).then_inc(s["picks_ready"], 1)
                    dve.wait_ge(s["picks_ready"], 6 * b + 5 + i)

            for step in range(-AHEAD, B + 4):
                if step == -1:
                    mod_rows()
                    dve.wait_ge(s["stack_zero1"], 2)
                    one_rows(slice(1, RING), "one_rows1")
                has = lambda b: 0 <= b < B
                for j in range(NPAIR):
                    if j == 1 and has(step - 3):
                        gate_attn(step - 3)
                    if j == 1 and step - 3 == B - 1:
                        x1_last(step - 3)
                    if j == 7 and has(step - 4):
                        top2(step - 4)
                    if j == 3 and has(step - 3):
                        ln2_stats(step - 3)
                    if j == 4 and step == -AHEAD:
                        split(0, 0)
                        split(0, 1)
                    if j == 4 and has(step + AHEAD):
                        values(step + AHEAD)
                    if j == 6 and has(step - 2):
                        normalise_attn(step - 2)
                    if has(step):
                        row_max(step, j)
                    if j == 0 and has(step - 1):
                        half_max(step - 1, 1)
                    if j == 1 and has(step + AHEAD + 1):
                        ln1_stats(step + AHEAD + 1)
                    if j == 3 and has(step):
                        half_max(step, 0)
                    if j == 4 and has(step - 3):
                        ln2_normalise(step - 3)
                    if j == 4 and step - 3 == B - 1:
                        h2_last(step - 3)
                    if j == 4 and has(step - 2):
                        pad_term(step - 2)
                    if j == 5 and step > -AHEAD and has(step + AHEAD):
                        split(step + AHEAD, 0)
                    if j == 6 and step > -AHEAD and has(step + AHEAD):
                        split(step + AHEAD, 1)
                    if j == 7 and has(step + AHEAD + 1):
                        normalise(step + AHEAD + 1)

            count = [0]

            def step_done(ins):
                count[0] += 1
                ins.then_inc(s["pos_steps"], 1)
                dve.wait_ge(s["pos_steps"], count[0])

            nc.vector.tensor_tensor(wts[:, 0, :], top[:, :, 1], top[:, :, 0], ALU.subtract).then_inc(s["wt_steps"], 1)
            dve.wait_ge(s["rank_ps"], 1)
            step_done(nc.vector.tensor_scalar(ntile_e[:, 0], psR[:, NT * E:(NT + 1) * E], P / 2 - 0.5, 1.0 / P, ALU.add, ALU.mult))
            step_done(nc.vector.tensor_scalar(ntile_e[:, 1], ntile_e[:, 0], ROUND, None, ALU.add))
            step_done(nc.vector.tensor_scalar(upto[:, 0, E:], ntile_e[:, 1], -ROUND, None, ALU.add))
            for i in range(3):
                d = 1 << i
                step_done(nc.vector.tensor_tensor(upto[:, i + 1, E:], upto[:, i, E:], upto[:, i, E - d:2 * E - d], ALU.add))
            step_done(nc.vector.scalar_tensor_tensor(
                out=place[:], in0=upto[:, 3:4, E - 1:2 * E - 1].broadcast_to([P, NT, E]), scalar=float(P),
                in1=psR[:, 0:NT * E].rearrange("p (t e) -> p t e", e=E), op0=ALU.mult, op1=ALU.add))
            for k in range(TOPK):
                last = nc.vector.tensor_tensor(picked[:, k], pick[:, k], place[:], ALU.mult)
            step_done(last)
            step_done(nc.vector.tensor_reduce(pos[:, 0].rearrange("p (k t) -> p k t", k=TOPK), picked[:], AX.X, ALU.add))
            step_done(nc.vector.tensor_scalar(pos[:, 1], pos[:, 0], 0.5 - P / 2, 1.0 / P, ALU.add, ALU.mult))
            step_done(nc.vector.tensor_scalar(pos[:, 2], pos[:, 1], ROUND, None, ALU.add))
            step_done(nc.vector.tensor_scalar(pos[:, 3], pos[:, 2], -ROUND, None, ALU.add))
            step_done(nc.vector.scalar_tensor_tensor(out=pos[:, 4], in0=pos[:, 3], scalar=-float(P), in1=pos[:, 0],
                                                     op0=ALU.mult, op1=ALU.add))
            nkt = TOPK * NT
            nc.vector.tensor_tensor(
                inv_sel[:], iota_a[:].rearrange("p (o a) -> p o a", o=1).broadcast_to([P, nkt, NTILE]),
                pos[:, 3].rearrange("p (k o) -> p k o", o=1).broadcast_to([P, nkt, NTILE]), ALU.is_equal).then_inc(s["sel_ready"], 1)
            for i in range(nkt):
                ins = nc.vector.tensor_scalar(inv_lhs[:, i], iota_c[:], pos[:, 4, i:i + 1], None, ALU.is_equal)
                ins.then_inc(s["lhs_ready"], 1)
            dve.wait_ge(s["inv_ps"], 1)
            row, kt = psM[:, 0:NTILE], psM[:, NTILE:2 * NTILE]
            step_done(nc.vector.tensor_copy(inv[:, 4], kt))
            step_done(nc.vector.scalar_tensor_tensor(out=inv[:, 0], in0=inv[:, 4], scalar=float(P), in1=row, op0=ALU.mult, op1=ALU.add))
            nc.vector.tensor_scalar(inv[:, 1], inv[:, 4], NT + 0.5, -float(NTOK), ALU.is_ge, ALU.mult)
            step_done(nc.vector.scalar_tensor_tensor(out=inv[:, 2], in0=inv[:, 4], scalar=0.5, in1=dump_row[:], op0=ALU.is_lt, op1=ALU.mult))
            step_done(nc.vector.scalar_tensor_tensor(out=inv[:, 3], in0=inv[:, 0], scalar=-float(P), in1=inv[:, 1], op0=ALU.add, op1=ALU.add))
            nc.vector.tensor_scalar(gat_idx[:], inv[:, 3], 0.0, None, ALU.max).then_inc(s["idx_ready"], 1)
            nc.vector.scalar_tensor_tensor(out=sca_idx[:], in0=inv[:, 0], scalar=-float(P), in1=inv[:, 2],
                                           op0=ALU.add, op1=ALU.add).then_inc(s["idx_ready"], 1)

            step_done(nc.vector.tensor_tensor(
                te_cmp[:], upto[0:1, 3:4, E:].broadcast_to([1, NTILE, E]),
                iota_a[0:1].rearrange("p (a o) -> p a o", o=1).broadcast_to([1, NTILE, E]), ALU.is_le))
            step_done(nc.vector.tensor_reduce(te_sum[:], te_cmp[:], AX.X, ALU.add))
            nc.vector.tensor_scalar(tile_e[:], te_sum[:], float(E - 1), None, ALU.min).then_inc(s["te_ready"], 1)
            dve.wait_ge(s["wt_exp"], 1)
            step_done(nc.vector.tensor_scalar(wts[:, 3, :], wts[:, 1, :], 1.0, None, ALU.add))
            step_done(nc.vector.reciprocal(wts[:, 2, :], wts[:, 3, :]))
            step_done(nc.vector.tensor_tensor(wts[:, 3, :], wts[:, 1, :], wts[:, 2, :], ALU.mult))

            def xsT_copy(n, r):
                dve.wait_ge(*((s["xsT_first"], 1) if first(n) else (s["xsT_ps"], n)))
                nc.vector.tensor_copy(xsT[:, r], psX).then_inc(s["xsT_ready"], 1)

            def gate_hidden(m, r):
                dve.wait_ge(s["silu_ready"], m + 1)
                dve.wait_ge(s["u_ps"], m + 1)
                nc.vector.tensor_tensor(hid[:, r], psU[r], gate_act[:, r], ALU.mult).then_inc(s["hid_ready"], 1)

            def expert(n):
                return dve.value_load(tile_e[0:1, bass.ds(n, 1)], min_val=0, max_val=E - 1)

            def w1_copy(n, r, e):
                nc.vector.tensor_copy(w1_t[:, r], w1_sb[:, bass.ds(e, 1), :].rearrange("c o i -> c (o i)"))

            def w2_copy(n, r, e):
                nc.vector.tensor_copy(w2_t[:, r], w2_sb[:, bass.ds(e, 1)].rearrange("p o k c -> p (o k c)"))

            dve.wait_ge(s["moe_w"], 16 * 3 * (E // 2))
            for r in range(2):
                w1_copy(r, r, expert(r))
                xsT_copy(r, r)
            for r in range(2):
                w2_copy(r, r, expert(r))
            gate_hidden(0, 0)

            def three_tiles(it):
                for r in range(TRING):
                    n = it * TRING + r
                    e = expert(n + 2)
                    if not first(n):
                        dve.wait_ge(s["u_ps"], n)
                    w1_copy(n + 2, (r + 2) % TRING, e)
                    xsT_copy(n + 2, (r + 2) % TRING)
                    gate_hidden(n + 1, (r + 1) % TRING)
                    w2_copy(n + 2, (r + 2) % TRING, e)

            three_tiles(0)
            with dve.Fori(1, rounds) as it:
                three_tiles(it)
            e = expert(NTILE - 1)
            dve.wait_ge(s["u_ps"], rounds * TRING)
            w1_copy(NTILE - 1, 2, e)
            xsT_copy(NTILE - 1, 2)
            gate_hidden(NTILE - 2, 1)
            w2_copy(NTILE - 1, 2, e)
            gate_hidden(NTILE - 1, 2)

            n = NT // 4
            for i in range(4):
                tt = slice(n * i, n * i + n)
                dve.wait_ge(s[f"y_in{i}"], 32)
                for j in range(n * i, n * i + n):
                    dve.wait_ge(s["y0_scaled"], j + 1)
                    ins = nc.vector.scalar_tensor_tensor(out=comb[:, j], in0=y01[:, 1, j], scalar=wts[:, 3, j:j + 1], in1=y01[:, 0, j],
                                                         op0=ALU.mult, op1=ALU.add)
                step_done(ins)
                v = comb[:, tt].rearrange("p (b t) c -> p b t c", t=2)
                ins = nc.vector.tensor_tensor(v, v, mod_sb[:, n * i // 2:n * (i + 1) // 2, 3:4, :].broadcast_to([P, n // 2, 2, C]), ALU.mult)
                if i < 3:
                    ins.then_inc(s["comb_ready"], 1)
                else:
                    step_done(ins)
                    nc.vector.tensor_tensor(outb[:, tt], comb[:, tt], x_sb[:, tt], ALU.add).then_inc(s["out_ready3"], 1)

        @block.tensor
        def _(pe):
            last_psM = [None]

            def take_psM(release, value):
                if last_psM[0]:
                    pe.wait_ge(*last_psM[0])
                last_psM[0] = (s[release], value)

            last_late = [(s["rowmax"], NPAIR * B)]

            def take_late(b, release, value):
                if b < B - 1:
                    take_psM(release, value)
                else:
                    pe.wait_ge(*last_late[0])
                    last_late[0] = (s[release], value)

            pe.wait_ge(s["consts"], 2)
            pe.wait_ge(s["c_in"], 16)
            nc.tensor.transpose(psM[:, 0:B], c_sb[:], ident[0:B, 0:B]).then_inc(s["cT_ps"], 1)
            pe.wait_ge(s["silu_c"], 1)
            pe.wait_ge(s["wmod_in0"], 16)
            for i in range(2):
                last = nc.tensor.matmul(psM[:, i * B:(i + 1) * B], wmod_sb[:, i * C:(i + 1) * C], cT[:, 3, :],
                                        start=True, stop=True)
            last.then_inc(s["modT_ps"], 1)
            take_psM("modT_ok", 2)

            def mod_matmul():
                pe.wait_ge(s["wmod_in1"], 32)
                nc.tensor.matmul(psO[0:B].rearrange("b h q -> b (h q)"), cT[:, 3, :], wmod_sb[:, 2 * C:6 * C],
                                 start=True, stop=True).then_inc(s["modrow_ps"], 1)

            def xn_T(b):
                pe.wait_ge(s["xn_ready"], b + 1)
                take_psM("hT_ready", b + 1)
                for t in range(2):
                    last = nc.tensor.transpose(psM[:, t * P:(t + 1) * P], xn[:, b % 2, t, :], ident[:])
                last.then_inc(s["xnT_ps"], 1)

            def project_qk(b):
                if b == 0:
                    pe.wait_ge(s["wqk_ok"], 2)
                take_psM("qkf_ready", 2 * b + 2)
                for i in range(2):
                    last = nc.tensor.matmul(psM[:, i * L:(i + 1) * L], wqk[:, i, :], hT[:], start=True, stop=True)
                last.then_inc(s["qk_ps"], 1)

            def project_v(b):
                take_psM("v_ready", b + 1)
                for t in range(2):
                    last = nc.tensor.matmul(psM[:, t * C:(t + 1) * C], hT[:, t * P:(t + 1) * P], wv_sb[:], start=True, stop=True)
                last.then_inc(s["v_ps"], 1)

            def scores_A(b, j):
                n = NPAIR * b + j
                if j == 0:
                    pe.wait_ge(stack_in[b % RING], 16 * NLOADS * (b // RING + 1))
                if n >= 2:
                    pe.wait_ge(s["rowmax"], n - 1)
                r = b % RING
                for qt in range(2):
                    nc.tensor.matmul(psA[:, n % 2, qt, :].rearrange("p (h k) -> p h k", h=H2),
                                     qs[0:SROWS, r, j, qt * P:(qt + 1) * P], kd[0:SROWS, r, :, j, :], start=True, stop=False)
                    off = (1 - qt) * P
                    last = nc.tensor.matmul(psA[:, n % 2, qt, :].rearrange("p (h k) -> p h k", h=H2)[:, :, off:off + P],
                                            ident_b[:], mask_b[:, qt], start=False, stop=True)
                last.then_inc(s["scoresA"], 1)

            def max_T(b, half):
                pe.wait_ge(s["half_max"], 2 * b + half + 1)
                take_psM("mT_ready", 2 * b + half + 1)
                pb = psM[0:8, 0:P].bitcast(BF16)
                for qt in range(2):
                    last = nc.tensor.transpose(pb[:, qt * P:(qt + 1) * P],
                                               negmb[:, b % 2, half, qt].rearrange("p h q -> p (h q)"), ident_b[:])
                last.then_inc(s["mT_ps"], 1)

            def scores_B(b, j, kt):
                n = NPAIR * b + j
                r = b % RING
                if j % 4 == 0 and kt == 0:
                    pe.wait_ge(s[f"m_in{j // 4}"], 16 * (b + 1))
                if n >= 1:
                    pe.wait_ge(s["exped"], 2 * n + kt - 1)
                for h in range(H2):
                    last = nc.tensor.matmul(psB[:, kt, h * L:(h + 1) * L], kd[:, r, h, j, kt * P:(kt + 1) * P],
                                            qs[:, r, j, :], start=True, stop=True)
                last.then_inc(s["scoresB"], 1)

            def weigh_values(b, i):
                half, piece = i // 4, i % 4
                h, kt = piece // 2, piece % 2
                if piece == 0:
                    pe.wait_ge(s["masked"], 8 * b + 4 * half + 4)
                    if half == 0:
                        pe.wait_ge(s["v_ready"], b + 1)
                    if half == 0 and b >= 1:
                        pe.wait_ge(s["o_ready"], b)
                    if half == 0 and b == 0:
                        pe.wait_ge(s["mod_steps"], 5)
                for g in range(4):
                    j = 4 * half + g
                    last = nc.tensor.matmul(psO[32 * g:32 * g + 32, half, :], vx[:, b % VRING, kt, j, h, :],
                                            probs[:, kt, j, h, :], start=(piece == 0), stop=(piece == 3))
                last.then_inc(s["pv"], 1)

            def o_T(b):
                pe.wait_ge(s["o_ready"], b + 1)
                take_late(b, "normed", b + 1)
                for qt in range(2):
                    for half in range(2):
                        i = 2 * qt + half
                        last = nc.tensor.transpose(late(b)[:, i * P:(i + 1) * P], oS[:, half, qt * P:(qt + 1) * P], ident[:])
                last.then_inc(s["oT_ps"], 1)

            def attn_T(b):
                take_late(b, "aT_ready", b + 1)
                for t in range(2):
                    last = nc.tensor.transpose(late(b)[:, t * P:(t + 1) * P], attn[:, t, :], ident[:])
                last.then_inc(s["aT_ps"], 1)

            def project_out(b):
                if b == 0:
                    pe.wait_ge(s["wo_in"], 32)
                take_late(b, "t1_ready", 2 * b + 2)
                for t in range(2):
                    last = nc.tensor.matmul(late(b)[:, t * C:(t + 1) * C], aT[:, t * P:(t + 1) * P], wo_sb[:], start=True, stop=True)
                last.then_inc(s["op_ps"], 1)

            def h2_T(b):
                pe.wait_ge(s["h2_ready"], b + 1)
                take_late(b, "h2T_ready", b + 1)
                for t in range(2):
                    last = nc.tensor.transpose(late(b)[:, t * P:(t + 1) * P], h2[:, b % 2, t, :], ident[:])
                last.then_inc(s["h2T_ps"], 1)

            def logits(b):
                take_late(b, "lg_ready", b + 1)
                for t in range(2):
                    last = nc.tensor.matmul(late(b)[:, 8 * t:8 * t + 8], h2T[:, t * P:(t + 1) * P], gate_sb[:], start=True, stop=True)
                last.then_inc(s["lg_ps"], 1)

            for step in range(-AHEAD, B + 4):
                if step == -1:
                    mod_matmul()
                a, nxt, prev = step, step + AHEAD, step - 1
                has = lambda b: 0 <= b < B
                for j in range(NPAIR):
                    if j == 1 and has(step - 3):
                        project_out(step - 3)
                    if j == 2 and has(prev):
                        max_T(prev, 1)
                    if j == 7 and has(step - 2):
                        attn_T(step - 2)
                    if j == 7 and step > B and has(step - 4):
                        logits(step - 4)
                    if has(a):
                        scores_A(a, j)
                    if j == 0 and has(nxt):
                        xn_T(nxt)
                    if has(prev):
                        scores_B(prev, j, 0)
                    if j == 6 and step <= B and has(step - 4):
                        logits(step - 4)
                    if j == 2 and has(nxt):
                        project_qk(nxt)
                    if j == 3 and has(nxt):
                        project_v(nxt)
                    if j == 4 and has(a):
                        max_T(a, 0)
                    if j == 5 and has(step - 2):
                        o_T(step - 2)
                    if j == 7 and has(step - 3):
                        h2_T(step - 3)
                    if has(prev):
                        scores_B(prev, j, 1)
                    for i in {5: (0, 1), 6: (2,), 7: (3,)}.get(j, ()):
                        if has(prev):
                            weigh_values(prev, i)
                    for i in {1: (4,), 2: (5, 6), 3: (7,)}.get(j, ()):
                        if has(prev - 1):
                            weigh_values(prev - 1, i)

            pe.wait_ge(s["picks_ready"], 6 * B)
            rank = psR[:, 0:NT * E]
            pe.wait_ge(s["exped"], 2 * NPAIR * B)
            nc.tensor.matmul(rank, tri[:], used[:].rearrange("p t e -> p (t e)"), start=True, stop=False)
            nc.tensor.matmul(rank, ones_b[:], before[:, 0:NT].rearrange("p t e -> p (t e)"), start=False, stop=True)
            nc.tensor.matmul(psR[:, NT * E:(NT + 1) * E], ones_b[:], before[:, NT], start=True, stop=True).then_inc(s["rank_ps"], 1)
            pe.wait_ge(*last_psM[0])
            nkt = TOPK * NT
            pe.wait_ge(s["rhs0_ready"], 1)
            pe.wait_ge(s["rhs1_ready"], 1)
            for i in range(nkt):
                pe.wait_ge(s["lhs_ready"], i + 1)
                last = nc.tensor.matmul(psM[:, 0:2 * NTILE].rearrange("p (w a) -> p w a", w=2), inv_lhs[:, i],
                                        inv_rhs[:, :, i, :], start=(i == 0), stop=(i == nkt - 1))
            last.then_inc(s["inv_ps"], 1)

            pe.wait_ge(s["moe_w"], 16 * 3 * (E // 2))
            pe.wait_ge(s["te_ready"], 1)
            pe.wait_ge(s["idx_ready"], 2)

            def xs_T(n, r, turn, done="xsT_ps"):
                pe.wait_ge(gathered[r], 16 * (turn + 1))
                nc.tensor.transpose(psX, xs[:, r], ident[:]).then_inc(s[done], 1)

            def up(m, r):
                pe.wait_ge(s["xsT_ready"], m + 1)
                for ps, w, done in ((psG[r], w1_t, "g_ps"), (psU[r], w3_t, "u_ps")):
                    if done == "u_ps":
                        pe.wait_ge(s["w3_ready"], m + 1)
                    for k in range(NC):
                        last = nc.tensor.matmul(ps[:, k * P:(k + 1) * P], w[:, r, k * P:(k + 1) * P],
                                                xsT[:, r], start=True, stop=True)
                    last.then_inc(s[done], 1)

            def down(n, r):
                pe.wait_ge(s["hid_ready"], n + 1)
                if not first(n):
                    pe.wait_ge(s["y_ready"], n)
                for k in range(NC):
                    last = nc.tensor.matmul(psY, hid[:, r, k * P:(k + 1) * P], w2_t[:, r, k * C:(k + 1) * C],
                                            start=(k == 0), stop=(k == NC - 1))
                last.then_inc(s["y_ps"], 1)

            xs_T(0, 0, 0, "xsT_first")
            pe.wait_ge(s["xsT_ready"], 1)
            xs_T(1, 1, 0)
            up(0, 0)

            def three_tiles(it):
                for r in range(TRING):
                    n = it * TRING + r
                    up(n + 1, (r + 1) % TRING)
                    xs_T(n + 2, (r + 2) % TRING, it + (r + 2) // TRING)
                    down(n, r)

            three_tiles(0)
            with pe.Fori(1, rounds) as it:
                three_tiles(it)
            for r in range(TRING):
                n = rounds * TRING + r
                if r < TRING - 1:
                    up(n + 1, r + 1)
                if r < TRING - 2:
                    xs_T(n + 2, r + 2, rounds)
                down(n, r)


_INS = ("L0_attn_x", "L0_attn_wq", "L0_attn_bq", "L0_attn_wk", "L0_attn_bk", "L0_attn_wv", "L0_attn_bv", "L0_attn_wo", "L0_attn_bo",
        "L0_ffn_gate", "L0_ffn_experts_w1", "L0_ffn_experts_w2", "L0_ffn_experts_w3", "L0_c", "L0_wmod")


def kernel(**inputs):
    import numpy as _np
    import concourse.bacc as _bacc
    from concourse import mybir as _mybir
    from concourse.bass_utils import run_bass_kernel_spmd as _run

    nc = _bacc.Bacc("TRN2", target_bir_lowering=False, num_devices=1)
    arrays, args = {}, []
    for name in _INS:
        a = _np.ascontiguousarray(inputs[name])
        arrays[f"in_{name}_dram"] = a
        args.append(nc.dram_tensor(f"in_{name}_dram", a.shape, _mybir.dt.from_np(a.dtype), kind="ExternalInput").ap())
    shape = inputs["L0_attn_x"].shape
    out = nc.dram_tensor("out_0_dram", shape, _mybir.dt.float32, kind="ExternalOutput").ap()
    adaln_attention_moe(nc, *args, out)
    r = _run(nc, [arrays], core_ids=[0])
    return r.results[0]["out_0_dram"]
```
